# Optimizing a Trainium2 kernel written in Bass

```python
import numpy as np
import jax
import jax.numpy as jnp

def _softmax(x, axis=-1):
    return jax.nn.softmax(x, axis=axis)

def _gelu(x):
    return jax.nn.gelu(x, approximate=True)

def _silu(x):
    return jax.nn.silu(x)

def _sigmoid(x):
    return jax.nn.sigmoid(x)

def _layernorm(x, axis=-1, eps=1e-05):
    m = jnp.mean(x, axis=axis, keepdims=True)
    v = jnp.var(x, axis=axis, keepdims=True)
    return (x - m) / jnp.sqrt(v + eps)

def _scatter_add(tgt, idx, src, axis=0):
    return tgt.at[idx].add(src)

def _segment_sum(src, seg, n):
    return jax.ops.segment_sum(src, seg, n)
kernel_name = 'mk_seq_postln_d1_jaxref_r4_da0119'

def setup_inputs(seed: int=0):
    np.random.seed(seed)
    _w = jnp.asarray

    def _L0_attn_setup():
        import jax, jax.numpy as jnp
        import numpy as np
        B, S, H, NH = (2, 512, 256, 16)
        D = H // NH
        FF = 4 * H

        def _layernorm(x, g, b, eps=1e-05):
            mu = jnp.mean(x, axis=-1, keepdims=True)
            var = jnp.mean((x - mu) ** 2, axis=-1, keepdims=True)
            return (x - mu) * jax.lax.rsqrt(var + eps) * g + b

        def _attention(x, wq, bq, wk, bk, wv, bv, wo, bo):
            b, s, _ = x.shape
            q = (x @ wq.T + bq).reshape(b, s, NH, D).transpose(0, 2, 1, 3)
            k = (x @ wk.T + bk).reshape(b, s, NH, D).transpose(0, 2, 1, 3)
            v = (x @ wv.T + bv).reshape(b, s, NH, D).transpose(0, 2, 1, 3)
            scores = jnp.einsum('bhqd,bhkd->bhqk', q, k) / jnp.sqrt(jnp.float32(D))
            causal = jnp.tril(jnp.ones((s, s), jnp.float32))
            att = jax.nn.relu(scores) * causal
            att = att / (jnp.sum(att, axis=-1, keepdims=True) + 1e-09)
            ctx = jnp.einsum('bhqk,bhkd->bhqd', att, v)
            ctx = ctx.transpose(0, 2, 1, 3).reshape(b, s, H)
            return ctx @ wo.T + bo
        key = jax.random.key(seed)
        ks = jax.random.split(key, 20)

        def lin(k, o, i, scale=0.02):
            return jax.random.normal(k, (o, i), jnp.float32) * scale
        inp = {'x': jax.random.normal(ks[0], (B, S, H), jnp.float32), 'sf_w': lin(ks[1], H, H, 0.01), 'sf_b': jnp.zeros((H,), jnp.float32), 'mask': jax.random.bernoulli(ks[2], 0.1, (H, H)).astype(jnp.float32), 'wq': lin(ks[3], H, H), 'bq': jnp.zeros((H,), jnp.float32), 'wk': lin(ks[4], H, H), 'bk': jnp.zeros((H,), jnp.float32), 'wv': lin(ks[5], H, H), 'bv': jnp.zeros((H,), jnp.float32), 'wo': lin(ks[6], H, H), 'bo': jnp.zeros((H,), jnp.float32), 'ff1_w': lin(ks[7], FF, H), 'ff1_b': jnp.zeros((FF,), jnp.float32), 'ff2_w': lin(ks[8], H, FF), 'ff2_b': jnp.zeros((H,), jnp.float32), 'g1': jnp.ones((H,), jnp.float32), 'b1': jnp.zeros((H,), jnp.float32), 'g2': jnp.ones((H,), jnp.float32), 'b2': jnp.zeros((H,), jnp.float32), 'g3': jnp.ones((H,), jnp.float32), 'b3': jnp.zeros((H,), jnp.float32)}
        return inp
    _L0_attn_in = _L0_attn_setup()

    def _L0_ffn_setup():
        import jax, jax.numpy as jnp
        import numpy as np
        E, D, F = (8, 256, 1024)
        B, S = (4, 512)

        def _layernorm(x, g, b, eps=1e-05):
            mu = jnp.mean(x, axis=-1, keepdims=True)
            var = jnp.var(x, axis=-1, keepdims=True)
            return (x - mu) * jax.lax.rsqrt(var + eps) * g + b
        key = jax.random.key(seed)
        ks = jax.random.split(key, 5)
        return {'input_features': jax.random.normal(ks[0], (B, S, D), jnp.float32), 'centroids': jax.random.normal(ks[1], (E, D), jnp.float32) * 0.1, 'ln_g': jnp.ones((E, D), jnp.float32), 'ln_b': jnp.zeros((E, D), jnp.float32), 'w1': jax.random.normal(ks[2], (E, F, D), jnp.float32) * (1.0 / np.sqrt(D).astype(np.float32)), 'b1': jnp.zeros((E, F), jnp.float32), 'w2': jax.random.normal(ks[3], (E, D, F), jnp.float32) * (1.0 / np.sqrt(F).astype(np.float32)), 'b2': jnp.zeros((E, D), jnp.float32)}
    _L0_ffn_in = _L0_ffn_setup()
    _d = {'L0_attn_x': _L0_attn_in['x'], 'L0_attn_sf_w': _L0_attn_in['sf_w'], 'L0_attn_sf_b': _L0_attn_in['sf_b'], 'L0_attn_mask': _L0_attn_in['mask'], 'L0_attn_wq': _L0_attn_in['wq'], 'L0_attn_bq': _L0_attn_in['bq'], 'L0_attn_wk': _L0_attn_in['wk'], 'L0_attn_bk': _L0_attn_in['bk'], 'L0_attn_wv': _L0_attn_in['wv'], 'L0_attn_bv': _L0_attn_in['bv'], 'L0_attn_wo': _L0_attn_in['wo'], 'L0_attn_bo': _L0_attn_in['bo'], 'L0_attn_ff1_w': _L0_attn_in['ff1_w'], 'L0_attn_ff1_b': _L0_attn_in['ff1_b'], 'L0_attn_ff2_w': _L0_attn_in['ff2_w'], 'L0_attn_ff2_b': _L0_attn_in['ff2_b'], 'L0_attn_g1': _L0_attn_in['g1'], 'L0_attn_b1': _L0_attn_in['b1'], 'L0_attn_g2': _L0_attn_in['g2'], 'L0_attn_b2': _L0_attn_in['b2'], 'L0_attn_g3': _L0_attn_in['g3'], 'L0_attn_b3': _L0_attn_in['b3'], 'L0_ffn_centroids': _L0_ffn_in['centroids'], 'L0_ffn_ln_g': _L0_ffn_in['ln_g'], 'L0_ffn_ln_b': _L0_ffn_in['ln_b'], 'L0_ffn_w1': _L0_ffn_in['w1'], 'L0_ffn_b1': _L0_ffn_in['b1'], 'L0_ffn_w2': _L0_ffn_in['w2'], 'L0_ffn_b2': _L0_ffn_in['b2']}
    _x0 = _d['L0_attn_x']
    _d['L0_attn_x'] = jax.random.normal(jax.random.fold_in(jax.random.key(seed), 1), (8, 512, 256), dtype=_x0.dtype)
    del _x0
    return _d

def reference(L0_attn_x, L0_attn_sf_w, L0_attn_sf_b, L0_attn_mask, L0_attn_wq, L0_attn_bq, L0_attn_wk, L0_attn_bk, L0_attn_wv, L0_attn_bv, L0_attn_wo, L0_attn_bo, L0_attn_ff1_w, L0_attn_ff1_b, L0_attn_ff2_w, L0_attn_ff2_b, L0_attn_g1, L0_attn_b1, L0_attn_g2, L0_attn_b2, L0_attn_g3, L0_attn_b3, L0_ffn_centroids, L0_ffn_ln_g, L0_ffn_ln_b, L0_ffn_w1, L0_ffn_b1, L0_ffn_w2, L0_ffn_b2):

    def _L0_attn_ref(x, sf_w, sf_b, mask, wq, bq, wk, bk, wv, bv, wo, bo, ff1_w, ff1_b, ff2_w, ff2_b, g1, b1, g2, b2, g3, b3):
        import jax, jax.numpy as jnp
        import numpy as np
        B, S, H, NH = (2, 512, 256, 16)
        D = H // NH
        FF = 4 * H

        def _layernorm(x, g, b, eps=1e-05):
            mu = jnp.mean(x, axis=-1, keepdims=True)
            var = jnp.mean((x - mu) ** 2, axis=-1, keepdims=True)
            return (x - mu) * jax.lax.rsqrt(var + eps) * g + b

        def _attention(x, wq, bq, wk, bk, wv, bv, wo, bo):
            b, s, _ = x.shape
            q = (x @ wq.T + bq).reshape(b, s, NH, D).transpose(0, 2, 1, 3)
            k = (x @ wk.T + bk).reshape(b, s, NH, D).transpose(0, 2, 1, 3)
            v = (x @ wv.T + bv).reshape(b, s, NH, D).transpose(0, 2, 1, 3)
            scores = jnp.einsum('bhqd,bhkd->bhqk', q, k) / jnp.sqrt(jnp.float32(D))
            causal = jnp.tril(jnp.ones((s, s), jnp.float32))
            att = jax.nn.relu(scores) * causal
            att = att / (jnp.sum(att, axis=-1, keepdims=True) + 1e-09)
            ctx = jnp.einsum('bhqk,bhkd->bhqd', att, v)
            ctx = ctx.transpose(0, 2, 1, 3).reshape(b, s, H)
            return ctx @ wo.T + bo
        out = _layernorm(x, g1, b1)
        out = out @ (sf_w * mask).T + sf_b
        x = x + out
        out = _layernorm(x, g2, b2)
        out = _attention(out, wq, bq, wk, bk, wv, bv, wo, bo)
        x = x + out
        out = _layernorm(x, g3, b3)
        out = jax.nn.relu(out @ ff1_w.T + ff1_b)
        out = out @ ff2_w.T + ff2_b
        return x + out

    def _L0_ffn_ref(input_features, centroids, ln_g, ln_b, w1, b1, w2, b2):
        import jax, jax.numpy as jnp
        import numpy as np
        E, D, F = (8, 256, 1024)
        B, S = (4, 512)

        def _layernorm(x, g, b, eps=1e-05):
            mu = jnp.mean(x, axis=-1, keepdims=True)
            var = jnp.var(x, axis=-1, keepdims=True)
            return (x - mu) * jax.lax.rsqrt(var + eps) * g + b
        Bf, Sf, Df = input_features.shape
        x = input_features.reshape(-1, Df)
        aff = x @ centroids.T
        assign = jnp.argmax(aff, axis=1)
        order = jnp.argsort(assign)
        xs = x[order]
        es = assign[order]
        alpha = jax.nn.sigmoid(jnp.take_along_axis(aff[order], es[:, None], axis=1))
        nE = centroids.shape[0]
        y = jnp.zeros_like(xs)
        for e in range(nE):
            h = _layernorm(xs, ln_g[e], ln_b[e])
            h = jax.nn.relu(h @ w1[e].T + b1[e])
            ye = xs + h @ w2[e].T + b2[e]
            y = y + jnp.where((es == e)[:, None], ye, 0.0)
        out_sorted = alpha * y + (1.0 - alpha) * xs
        inv = jnp.argsort(order)
        return out_sorted[inv].reshape(Bf, Sf, Df)
    x = L0_attn_x
    x = _layernorm(x + _L0_attn_ref(x, L0_attn_sf_w, L0_attn_sf_b, L0_attn_mask, L0_attn_wq, L0_attn_bq, L0_attn_wk, L0_attn_bk, L0_attn_wv, L0_attn_bv, L0_attn_wo, L0_attn_bo, L0_attn_ff1_w, L0_attn_ff1_b, L0_attn_ff2_w, L0_attn_ff2_b, L0_attn_g1, L0_attn_b1, L0_attn_g2, L0_attn_b2, L0_attn_g3, L0_attn_b3), axis=-1)
    x = _layernorm(x + _L0_ffn_ref(x, L0_ffn_centroids, L0_ffn_ln_g, L0_ffn_ln_b, L0_ffn_w1, L0_ffn_b1, L0_ffn_w2, L0_ffn_b2), axis=-1)
    return x

_drawn_inputs = setup_inputs


def setup_inputs(seed=0):
    import zlib

    import numpy as np

    out = dict(_drawn_inputs(seed))
    spreads = {'L0_attn_sf_b': (0.0, 0.1),
     'L0_attn_bq': (0.0, 0.373),
     'L0_attn_bk': (0.0, 0.648),
     'L0_attn_bv': (0.0, 0.1),
     'L0_attn_bo': (0.0, 0.1),
     'L0_attn_ff1_b': (0.0, 0.1),
     'L0_attn_ff2_b': (0.0, 0.1),
     'L0_attn_g1': (1.0, 0.6),
     'L0_attn_b1': (0.0, 0.354),
     'L0_attn_g2': (1.0, 0.6),
     'L0_attn_b2': (0.0, 0.1),
     'L0_attn_g3': (1.0, 0.2),
     'L0_attn_b3': (0.0, 0.1),
     'L0_ffn_ln_g': (1.0, 0.2),
     'L0_ffn_ln_b': (0.0, 0.271),
     'L0_ffn_b1': (0.0, 0.269),
     'L0_ffn_b2': (0.0, 0.1)}
    factors = {}
    for name, (base, spread) in spreads.items():
        noise = np.random.default_rng([zlib.crc32(name.encode()), seed]).standard_normal(out[name].shape)
        drawn = base * np.exp(spread * noise) if base else spread * noise
        out[name] = jnp.asarray(drawn.astype(out[name].dtype))
    for name, factor in factors.items():
        out[name] = (out[name] * factor).astype(out[name].dtype)
    return out
```

```python
from contextlib import ExitStack

import concourse.bass as bass
from concourse import mybir

ALU = mybir.AluOpType
ACT = mybir.ActivationFunctionType
AX = mybir.AxisListType
F32 = mybir.dt.float32
BF16 = mybir.dt.bfloat16
I32 = mybir.dt.int32
U32 = mybir.dt.uint32

P = 128
NB, S, H = 8, 512, 256
NT = S // P
KD = H // P
NH, D = 16, 16
FF = 4 * H
FM = FF // P
NG = 4
NE = 8
N_TOK = NB * S
N_SLOT = (N_TOK + NE * (P - 1)) // P
XW = H + 4
EPS = 1e-5
UN = 3
assert N_SLOT % UN == 0

C_G1, C_B1, C_G2, C_B2, C_G3, C_B3, C_BQ, C_BK, C_F1B, C_ME, C_MO = 0, 2, 4, 6, 8, 10, 12, 14, 16, 24, 25
NCOL = 26
NCON = 2 * P + S + 2 * NT * NE + NT
NSLC = NE * 32 + NE * NE + N_SLOT * NE + N_SLOT
E_G, E_B, E_B1, E_B2 = 0, 2, 4, 12
EW = 12 + H


class Signal:

    def __init__(self, sem, per, step=1, ahead=0):
        self.sem, self.per, self.step, self.ahead = sem, per, step, ahead

    def inc(self, ins):
        return ins.then_inc(self.sem, self.step)

    def wait(self, eng, rnd, k=None):
        k = self.per if k is None else k
        value = rnd * (self.per * self.step) + (k + self.ahead) * self.step
        if isinstance(value, int) and value <= 0:
            return
        eng.wait_ge(self.sem, value)


class Chain:

    def __init__(self, eng, sem, per, ahead=0):
        self.eng, self.sem, self.per, self.k, self.ahead = eng, sem, per, 0, ahead

    def begin(self, rnd):
        self.rnd, self.k = rnd, self.ahead

    def link(self, ins):
        self.k += 1
        ins.then_inc(self.sem, 1)
        self.eng.wait_ge(self.sem, self.rnd * self.per + self.k)

    def end(self):
        assert self.k == self.per + self.ahead, (self.k, self.per)


def build(nc, x, sfw, sfm, wq, wk, wv, wo, ff1, ff2, cent, rows, cols, consts, slotc, w1, w2, epack, out):
    xs_dram = nc.dram_tensor("token_store", (N_TOK + P, XW), F32, kind="Internal").ap()
    table = nc.dram_tensor("slot_table", ((NE + 1) * N_TOK, 1), I32, kind="Internal").ap()
    ctx = ExitStack()
    with ctx:
        def sb(name, shape, dt=F32, stack=ctx):
            return stack.enter_context(nc.sbuf_tensor(name, shape, dt))

        def signal(name, per, step=1, ahead=0):
            return Signal(ctx.enter_context(nc.semaphore(name)), per, step, ahead)

        ps = ctx.enter_context(nc.psum_tensor("ps", [P, 8, 512], F32))

        w1_sb = sb("w1_sb", [P, NE * KD * FF])
        arena = sb("arena", [P, NE * FM * H])
        con = sb("con", [P, NCON])
        ident = con[:, 0:P]
        tri_u = con[:, P:2 * P]
        causal = con[:, 2 * P:2 * P + S]
        desc8 = con[:, 2 * P + S:2 * P + S + 32]
        ebase = con[:, 2 * P + S + 32:2 * P + S + 64]
        tok0 = con[:, 2 * P + S + 64:2 * P + S + 68]
        slc = sb("slc", [1, NSLC])
        nhalf = sb("nhalf", [P, NT])
        eps4 = sb("eps4", [P, NT])
        tab = sb("tab", [1, 3 * N_SLOT], I32)
        tabf = sb("tabf", [1, 3, N_SLOT])

        spare = sb("spare", [P, 4])
        s_load = signal("s_load", 5, 16)
        s_load_a = signal("s_load_a", 4, 16)
        s_load_f = signal("s_load_f", 4, 16)
        s_w1 = signal("s_w1", NE, 16)
        s_w2 = signal("s_w2", NE, 16)
        s_xstore = signal("s_xstore", 1, 16)
        s_scat = [signal(f"s_scat{t}", 1, 16, ahead=1) for t in range(NT)]
        s_pad = signal("s_pad", 1, 16)
        s_tab = signal("s_tab", 1)

        env = dict(ctx=ctx, w1_sb=w1_sb, con=con, ident=ident, tri_u=tri_u, causal=causal, desc8=desc8, ebase=ebase,
                   tok0=tok0, slc=slc, nhalf=nhalf, eps4=eps4, tab=tab, tabf=tabf, s_load=s_load, s_load_a=s_load_a,
                   s_load_f=s_load_f, arena=arena, spare=spare, s_w1=s_w1, s_w2=s_w2, s_xstore=s_xstore,
                   s_scat=s_scat, s_pad=s_pad, s_tab=s_tab, xs_dram=xs_dram, table=table, x=x, sfw=sfw, sfm=sfm,
                   wq=wq, wk=wk, wv=wv, wo=wo, ff1=ff1, ff2=ff2, cent=cent, rows=rows, cols=cols, consts=consts,
                   slotc=slotc, w1=w1, w2=w2, epack=epack, out=out)
        phase1 = ExitStack()
        with phase1:
            phase_1(nc, phase1, signal, sb, ps, env)
        phase2 = ExitStack()
        with phase2:
            phase_2(nc, phase2, signal, sb, ps, env)


def phase_1(nc, stack, signal, sb_, ps, g):
    def sb(name, shape, dt=F32):
        return sb_(name, shape, dt, stack)

    con, slc, nhalf, ident, tri_u, causal = g["con"], g["slc"], g["nhalf"], g["ident"], g["tri_u"], g["causal"]
    x, xs_dram, table = g["x"], g["xs_dram"], g["table"]
    s_xstore, s_scat, s_pad = g["s_xstore"], g["s_scat"], g["s_pad"]

    sfT = sb("sfT", [P, KD, H])
    wqT = sb("wqT", [P, KD, H])
    wkT = sb("wkT", [P, KD, H])
    wvT = sb("wvT", [P, KD, H])
    woT = sb("woT", [P, KD, H])
    ff1T = sb("ff1T", [P, KD, FF])
    ff2T = sb("ff2T", [P, FM, H])
    centT = sb("centT", [P, KD, NE])
    rowb = sb("rowb", [P, 4, H])
    col = sb("col", [P, NCOL])
    triu_b = sb("triu_b", [P, P], BF16)
    ones_b = sb("ones_b", [P, P], BF16)
    padid = sb("padid", [P, (NE + 1) * N_TOK // P], I32)
    zrow = sb("zrow", [P, XW])

    parts, at = {}, 0
    for name, size in (("xin", NT * H), ("xkf", NT * H), ("x1", NT * H), ("xh", NT * H), ("xT", KD * S), ("qT", KD * S),
                       ("kT", KD * 2 * S), ("vA", NT * NH * 32), ("att", 2 * 4 * S), ("num", S), ("ctxt", NT * H)):
        parts[name] = g["arena"][:, at:at + size]
        at += size
    assert at <= NE * FM * H

    def tiles(name):
        return parts[name].rearrange("p (t h) -> p t h", h=H)

    xin = tiles("xin")
    xkf = tiles("xkf")
    x1 = tiles("x1")
    xh = tiles("xh")
    ctxt = tiles("ctxt")
    xT = parts["xT"].rearrange("p (k s) -> p k s", k=KD)
    qT = parts["qT"].rearrange("p (k s) -> p k s", k=KD)
    kT = parts["kT"].rearrange("p (k g s) -> p k g s", k=KD, g=2)
    vA = parts["vA"].rearrange("p (t h c) -> p t h c", t=NT, h=NH)
    att = parts["att"].rearrange("p (b f s) -> p b f s", b=2, f=4)
    num = parts["num"]
    x2 = sb("x2", [P, NT, H])
    den = sb("den", [P, NT, 4])
    rden = sb("rden", [P, NT, 4])
    ctxT = xT
    xh3 = sb("xh3", [P, NT, H])
    xT3 = sb("xT3", [P, KD, S])
    hT = sb("hT", [P, FM, S])
    sfM = hT[:, 0, :].rearrange("p (k h) -> p k h", k=KD)
    r2 = sb("r2", [P, NT, H])
    x4 = sb("x4", [P, NT, XW])
    x4T = xT3
    aff = sb("aff", [P, NT, NE])
    ohf = sb("ohf", [P, NT, NE])
    amax2 = sb("amax2", [P, NT])
    oh = sb("oh", [P, NT, NE], BF16)
    cum = sb("cum", [P, NT + 1, NE], BF16)
    posf = sb("posf", [P, NT, NE])
    pos1 = sb("pos1", [P, NT])
    posi = sb("posi", [P, NT], U32)
    tokf = sb("tokf", [P, NT])
    toki = sb("toki", [P, NT], I32)
    tmp = sb("tmp", [1, N_SLOT * NE])
    cnt, til, end = sb("cnt", [1, NE]), sb("til", [1, NE]), sb("end", [1, NE])
    stats = {w: sb(f"st_{w}", [P, NT, 6]) for w in ("ln1", "ln2", "ln3", "ln4")}
    mv = {w: sb(f"mv_{w}", [P, NT, 2]) for w in stats}
    rstd = {w: sb(f"rs_{w}", [P, NT]) for w in stats}

    s_load, s_load_a, s_load_f = g["s_load"], g["s_load_a"], g["s_load_f"]
    spare, eps4 = g["spare"], g["eps4"]
    s_const = signal("s_const", 2)
    s_fill = signal("s_fill", 3)
    s_x = signal("s_x", 1, 16)
    s_pa = signal("s_pa", 1)
    s_pb = signal("s_pb", 1)
    s_var = {w: signal(f"s_var_{w}", 1) for w in stats}
    s_eps = {w: signal(f"s_eps_{w}", 1) for w in stats}
    s_rs = {w: signal(f"s_rs_{w}", 1) for w in stats}
    s_xh = {w: signal(f"s_xh_{w}", 1) for w in stats}
    s_T = {w: signal(f"s_T_{w}", 2) for w in stats}
    s_Te = {w: signal(f"s_Te_{w}", 1) for w in stats}
    s_Td = {w: signal(f"s_Td_{w}", 1) for w in stats}
    s_sf = signal("s_sf", 2)
    s_x1 = signal("s_x1", 2)
    s_xb2 = signal("s_xb2", 1)
    s_q = signal("s_q", 2)
    s_k = signal("s_k", 2)
    s_v = signal("s_v", 2)
    s_qe = signal("s_qe", 2)
    s_ke = signal("s_ke", 2)
    s_ve = signal("s_ve", 2)
    STEPS = NG * NT
    s_s = signal("s_s", STEPS)
    s_sa = signal("s_sa", STEPS)
    s_sm = signal("s_sm", STEPS)
    s_sd = signal("s_sd", STEPS)
    s_av = signal("s_av", STEPS)
    s_num = signal("s_num", NG)
    s_ct = signal("s_ct", NG)
    s_ctx = signal("s_ctx", NG)
    s_cT = signal("s_cT", 2)
    s_cTa = signal("s_cTa", 1)
    s_cTd = signal("s_cTd", 1)
    s_wo = signal("s_wo", 2)
    s_x2 = signal("s_x2", 2)
    s_r2 = signal("s_r2", 1)
    s_f1 = signal("s_f1", FM)
    s_f1e = signal("s_f1e", FM)
    s_f2 = signal("s_f2", 2)
    s_r3 = signal("s_r3", 2)
    s_af = signal("s_af", 1)
    s_afe = signal("s_afe", 1)
    s_oh = signal("s_oh", 1)
    s_rk = signal("s_rk", 1)
    s_pos = signal("s_pos", 1, ahead=1)
    s_cnt = signal("s_cnt", 1)
    sem_cm = g["ctx"].enter_context(nc.semaphore("chain_main"))
    sem_cf = g["ctx"].enter_context(nc.semaphore("chain_ffn"))
    sem_cr = g["ctx"].enter_context(nc.semaphore("chain_route"))
    sem_ct = g["ctx"].enter_context(nc.semaphore("chain_table"))
    sem_cp = g["ctx"].enter_context(nc.semaphore("chain_pool"))

    PER_MAIN = 3 + 2 * NG
    PER_FFN = 6 + NT
    PER_RANK = 3

    def row(k):
        return rowb[:, k, :].unsqueeze(1).broadcast_to([P, NT, H])

    def statistics(who, eng, b, w, src, chain):
        if who == "dve":
            for t in range(NT):
                last = eng.bn_stats(stats[w][:, t, :], src[:, t, 0:H])
            chain.link(last)
            eng.tensor_copy(spare[:, 1:2], spare[:, 0:1])
            for t in range(NT):
                last = eng.bn_aggr(mv[w][:, t, :], stats[w][:, t, :])
            s_var[w].inc(last)
        elif who == "pool":
            s_var[w].wait(eng, b)
            s_eps[w].inc(eng.tensor_tensor(rstd[w][:, :], mv[w][:, :, 1], eps4[:, 0:NT], ALU.add))
            s_eps[w].wait(eng, b)
            s_rs[w].inc(eng.tensor_tensor(rstd[w][:, :], rstd[w][:, :], nhalf[:, 0:NT], ALU.pow))

    def normalise(who, eng, b, w, src, dst, ready):
        if who == "dve":
            ready(eng)
            s_rs[w].wait(eng, b)
            for t in range(NT):
                last = eng.tensor_scalar(dst[:, t, 0:H], src[:, t, 0:H], mv[w][:, t, 0:1], rstd[w][:, t:t + 1],
                                         ALU.subtract, ALU.mult)
            s_xh[w].inc(last)

    def transposes(who, eng, b, w, src, dst, banks, gc=None, bc=None, second="act", free=None):
        if who == "pe":
            s_xh[w].wait(eng, b)
            if free:
                free(eng)
            for kd in range(KD):
                for t in range(NT):
                    last = eng.transpose(ps[:, banks[kd], t * P:(t + 1) * P], src[:, t, kd * P:(kd + 1) * P], ident)
                s_T[w].inc(last)
            return
        for kd, owner, sig in ((0, "act", s_Te[w]), (1, second, s_Td[w])):
            if who != owner:
                continue
            s_T[w].wait(eng, b, kd + 1)
            o, i = dst[:, kd, :], ps[:, banks[kd], :]
            if owner == "act":
                if gc is None:
                    sig.inc(eng.activation(o, i, ACT.Copy))
                else:
                    sig.inc(eng.activation(o, i, ACT.Identity, bias=col[:, bc + kd:bc + kd + 1],
                                           scale=col[:, gc + kd:gc + kd + 1]))
            elif gc is None:
                sig.inc(eng.tensor_copy(o, i))
            else:
                sig.inc(eng.tensor_scalar(o, i, col[:, gc + kd:gc + kd + 1], col[:, bc + kd:bc + kd + 1],
                                          ALU.mult, ALU.add))

    def load_x(who, eng, b):
        if who == "sp":
            s_pa.wait(eng, b - 1)
            s_pb.wait(eng, b - 1)
            s_xh["ln1"].wait(eng, b - 1)
            s_x.inc(eng.dma_start(xin[:, :, :], x[bass.ds(b * S, S), :].rearrange("(t p) h -> p t h", p=P)))

    def load_w1(who, eng, b):
        if who == "sp":
            g["s_w1"].inc(eng.dma_start(g["w1_sb"][:, bass.ds(b * (KD * FF), KD * FF)],
                                        g["w1"][bass.ds(b * P, P), :]))

    def pre_a(who, eng, b):
        if who == "pool":
            s_x.wait(eng, b)
            s_xh["ln2"].wait(eng, b - 1)
            s_pa.inc(eng.tensor_tensor(x1[:, :, :], xin[:, :, :], row(0), ALU.add))

    def pre_b(who, eng, b):
        if who == "pool":
            s_r2.wait(eng, b - 1)
            s_pb.inc(eng.tensor_tensor(xkf[:, :, :], xin[:, :, :], row(2), ALU.add))

    def ln1(who, eng, b, chain):
        if who == "dve":
            s_x.wait(eng, b)
        statistics(who, eng, b, "ln1", xin, chain)
        normalise(who, eng, b, "ln1", xin, xh, lambda e: s_T["ln2"].wait(e, b - 1))

    def ln1_T(who, eng, b):
        def free(e):
            s_cTa.wait(e, b - 1)
            s_cTd.wait(e, b - 1)
        if who == "act":
            s_wo.wait(eng, b - 1)
        transposes(who, eng, b, "ln1", xh, xT, (0, 1), C_G1, C_B1, "act", free)

    def sf(who, eng, b):
        if who == "pe":
            s_Te["ln1"].wait(eng, b)
            s_Td["ln1"].wait(eng, b)
            s_x2.wait(eng, b - 1)
            for t in range(NT):
                for kd in range(KD):
                    last = eng.matmul(ps[:, 2 + t // 2, (t % 2) * H:(t % 2) * H + H], xT[:, kd, t * P:(t + 1) * P],
                                      sfT[:, kd, :], start=kd == 0, stop=kd == KD - 1)
                if t % 2:
                    s_sf.inc(last)
        elif who == "dve":
            s_pa.wait(eng, b)
            for i in range(2):
                s_sf.wait(eng, b, i + 1)
                v = x1[:, 2 * i:2 * i + 2, :]
                s_x1.inc(eng.tensor_tensor(v, ps[:, 2 + i, :].rearrange("p (t h) -> p t h", t=2), v, ALU.add))
            s_x1.wait(eng, b)

    def pre2(who, eng, b):
        if who == "pool":
            s_x1.wait(eng, b)
            s_xh["ln3"].wait(eng, b - 1)
            s_r2.wait(eng, b - 1)
            s_xb2.inc(eng.tensor_tensor(x2[:, :, :], x1[:, :, :], row(1), ALU.add))

    def ln2(who, eng, b, chain):
        statistics(who, eng, b, "ln2", x1, chain)
        normalise(who, eng, b, "ln2", x1, xh, lambda e: s_T["ln1"].wait(e, b))

    def ln2_T(who, eng, b):
        def free(e):
            s_Te["ln1"].wait(e, b)
            s_Td["ln1"].wait(e, b)
        if who == "act":
            s_sf.wait(eng, b)
        transposes(who, eng, b, "ln2", xh, xT, (0, 1), C_G2, C_B2, "act", free)

    def qkv(who, eng, b):
        if who == "pe":
            if isinstance(b, int) and b == 0:
                g["s_load_a"].wait(eng, 0)
            s_Te["ln2"].wait(eng, b)
            s_Td["ln2"].wait(eng, b)
            for w, b0, free, sig in ((wqT, 2, s_x1, s_q), (wkT, 4, None, s_k)):
                for m in range(KD):
                    if m == 0 and free:
                        free.wait(eng, b)
                    if m == 0 and not free:
                        s_pos.wait(eng, b - 2)
                        s_ctx.wait(eng, b - 1)
                    for kd in range(KD):
                        last = eng.matmul(ps[:, b0 + m, :], w[:, kd, m * P:(m + 1) * P], xT[:, kd, :],
                                          start=kd == 0, stop=kd == KD - 1)
                    sig.inc(last)
            for t in range(NT):
                for kd in range(KD):
                    last = eng.matmul(ps[:, t // 2, (t % 2) * H:(t % 2) * H + H], xT[:, kd, t * P:(t + 1) * P],
                                      wvT[:, kd, :], start=kd == 0, stop=kd == KD - 1)
                if t % 2:
                    s_v.inc(last)
        elif who == "act":
            s_s.wait(eng, b - 1)
            for m in range(KD):
                s_q.wait(eng, b, m + 1)
                s_qe.inc(eng.activation(qT[:, m, :], ps[:, 2 + m, :], ACT.Identity, bias=col[:, C_BQ + m:C_BQ + m + 1]))
        elif who == "dve":
            s_s.wait(eng, b - 1)
            for m in range(KD):
                s_k.wait(eng, b, m + 1)
                for par, mask in ((0, C_ME), (1, C_MO)):
                    last = eng.tensor_scalar(kT[:, m, par, :], ps[:, 4 + m, :], col[:, C_BK + m:C_BK + m + 1],
                                             col[:, mask:mask + 1], ALU.add, ALU.mult)
                s_ke.inc(last)
            s_av.wait(eng, b - 1)
            for i in range(2):
                s_v.wait(eng, b, i + 1)
                for j in range(2):
                    last = eng.tensor_tensor(vA[:, 2 * i + j, :, 0:D],
                                             ps[:, i, j * H:(j + 1) * H].rearrange("p (h d) -> p h d", h=NH),
                                             rowb[:, 3, :].rearrange("p (h d) -> p h d", h=NH), ALU.add)
                s_ve.inc(last)

    def scores(who, eng, b, n):
        gt, gp, kt = n // 8, (n // 4) % 2, n % 4
        q0, w = kt * P, S - kt * P
        buf = n % 2
        if who == "pe":
            if n == 0:
                s_qe.wait(eng, b)
                s_ke.wait(eng, b)
                s_ve.wait(eng, b)
            else:
                s_sa.wait(eng, b, n)
                s_sd.wait(eng, b, n)
            for s in range(4):
                r = slice(32 * s, 32 * s + 32)
                last = eng.matmul(ps[:, s, q0:S], kT[r, gt, gp, q0:q0 + P], qT[r, gt, q0:S], start=True, stop=True)
            s_s.inc(last)
        elif who == "act":
            s_s.wait(eng, b, n + 1)
            s_av.wait(eng, b, n - 1)
            s_sa.inc(eng.activation(att[:, buf, 0:2, q0:S], ps[:, 0:2, q0:S], ACT.Relu))
        elif who == "pool":
            s_sa.wait(eng, b, n + 1)
            v = att[:, buf, 0:2, q0:q0 + P]
            s_sm.inc(eng.tensor_tensor(v, v, causal[:, 0:P].unsqueeze(1).broadcast_to([P, 2, P]), ALU.mult))
        elif who == "dve":
            s_s.wait(eng, b, n + 1)
            s_av.wait(eng, b, n - 1)
            for s in (2, 3):
                last = eng.scalar_tensor_tensor(out=att[:, buf, s, q0:S], in0=ps[:, s, q0:S], scalar=0.0,
                                                in1=causal[:, 0:w], op0=ALU.max, op1=ALU.mult)
            s_sd.inc(last)

    def weigh(who, eng, b, n):
        if who != "pe":
            return
        gt, gp, kt = n // 8, (n // 4) % 2, n % 4
        q0, buf = kt * P, n % 2
        s_sm.wait(eng, b, n + 1)
        s_sd.wait(eng, b, n + 1)
        if n == 0:
            s_ke.wait(eng, b)
        elif kt == 0:
            s_num.wait(eng, b, n // 4)
        for s in range(4):
            head = 8 * gt + 2 * s + gp
            last = eng.matmul(ps[32 * s:32 * s + 32, 4, q0:S], vA[:, kt, head, :], att[:, buf, s, q0:S],
                              start=kt == 0, stop=kt == NT - 1)
        s_av.inc(last)

    def group_out(who, eng, b, grp, chain):
        gt, gp = grp // 2, grp % 2
        if who == "act":
            s_av.wait(eng, b, 4 * grp + 4)
            if grp == 0:
                s_ct.wait(eng, b - 1)
            else:
                s_ct.wait(eng, b, grp)
            s_num.inc(eng.activation(num[:, :], ps[:, 4, :], ACT.Copy))
        elif who == "pe":
            s_num.wait(eng, b, grp + 1)
            if grp:
                s_ctx.wait(eng, b, grp)
            for t in range(NT):
                last = eng.transpose(ps[:, 5, t * P:(t + 1) * P], num[:, t * P:(t + 1) * P], ident)
            s_ct.inc(last)
        elif who == "dve":
            s_ct.wait(eng, b, grp + 1)
            v = ps[:, 5, :].rearrange("p (t s c) -> p t s c", t=NT, s=4)
            chain.link(eng.tensor_scalar(den[:, :, :], v[:, :, :, D], 1e-9, None, ALU.add))
            chain.link(eng.reciprocal(rden[:, :, :], den[:, :, :]))
            if grp == 0:
                s_cT.wait(eng, b - 1)
            o = ctxt[:, :, :].rearrange("p t (g s q d) -> p g q t s d", g=2, s=4, q=2)
            for t in range(NT):
                last = eng.tensor_tensor(o[:, gt, gp, t], v[:, t, :, 0:D],
                                         rden[:, t, :].unsqueeze(2).broadcast_to([P, 4, D]), ALU.mult)
            s_ctx.inc(last)

    def ctx_T(who, eng, b):
        if who == "pe":
            s_ctx.wait(eng, b)
            s_sa.wait(eng, b)
            for kd in range(KD):
                for t in range(NT):
                    last = eng.transpose(ps[:, kd, t * P:(t + 1) * P], ctxt[:, t, kd * P:(kd + 1) * P], ident)
                s_cT.inc(last)
        elif who == "act":
            s_cT.wait(eng, b, 1)
            s_wo.wait(eng, b - 1)
            s_cTa.inc(eng.activation(ctxT[:, 0, :], ps[:, 0, :], ACT.Copy))
        elif who == "dve":
            s_cT.wait(eng, b, 2)
            s_wo.wait(eng, b - 1)
            s_cTd.inc(eng.tensor_copy(ctxT[:, 1, :], ps[:, 1, :]))

    def proj_o(who, eng, b):
        if who == "pe":
            s_cTa.wait(eng, b)
            s_cTd.wait(eng, b)
            s_sd.wait(eng, b)
            for t in range(NT):
                for kd in range(KD):
                    last = eng.matmul(ps[:, 2 + t // 2, (t % 2) * H:(t % 2) * H + H], ctxT[:, kd, t * P:(t + 1) * P],
                                      woT[:, kd, :], start=kd == 0, stop=kd == KD - 1)
                if t % 2:
                    s_wo.inc(last)
        elif who == "dve":
            s_xb2.wait(eng, b)
            for i in range(2):
                s_wo.wait(eng, b, i + 1)
                v = x2[:, 2 * i:2 * i + 2, :]
                s_x2.inc(eng.tensor_tensor(v, ps[:, 2 + i, :].rearrange("p (t h) -> p t h", t=2), v, ALU.add))
            s_x2.wait(eng, b)

    def residual2(who, eng, b):
        if who == "pool":
            s_x2.wait(eng, b)
            s_xh["ln4"].wait(eng, b - 1)
            s_r2.inc(eng.tensor_tensor(r2[:, :, :], xkf[:, :, :], x2[:, :, :], ALU.add))

    def ln3(who, eng, b, chain):
        statistics(who, eng, b, "ln3", x2, chain)
        normalise(who, eng, b, "ln3", x2, xh3, lambda e: s_T["ln3"].wait(e, b - 1))

    def ln3_T(who, eng, b):
        def free(e):
            s_afe.wait(e, b - 1)
            s_Td["ln4"].wait(e, b - 1)
        if who in ("act", "dve"):
            s_af.wait(eng, b - 1)
        transposes(who, eng, b, "ln3", xh3, xT3, (6, 7), C_G3, C_B3, "act", free)

    def ffn1(who, eng, b, m):
        if who == "pe":
            if m == 0:
                s_Te["ln3"].wait(eng, b)
                s_Td["ln3"].wait(eng, b)
            if m >= 2:
                s_f1e.wait(eng, b, m - 1)
            for kd in range(KD):
                last = eng.matmul(ps[:, 6 + m % 2, :], ff1T[:, kd, m * P:(m + 1) * P], xT3[:, kd, :],
                                  start=kd == 0, stop=kd == KD - 1)
            s_f1.inc(last)
        elif who == "act":
            s_f1.wait(eng, b, m + 1)
            if m == 0:
                s_f2.wait(eng, b - 1)
            s_f1e.inc(eng.activation(hT[:, m, :], ps[:, 6 + m % 2, :], ACT.Relu,
                                     bias=col[:, C_F1B + m:C_F1B + m + 1]))

    def ffn2(who, eng, b, t, half):
        if who == "pe":
            if t == 0 and half == 0:
                s_f1e.wait(eng, b)
            for m in range(4 * half, 4 * half + 4):
                last = eng.matmul(ps[:, 6 + t // 2, (t % 2) * H:(t % 2) * H + H], hT[:, m, t * P:(t + 1) * P],
                                  ff2T[:, m, :], start=m == 0, stop=m == FM - 1)
            if t % 2 and half:
                s_f2.inc(last)
        elif who == "dve" and t % 2 and half:
            i = t // 2
            s_f2.wait(eng, b, i + 1)
            s_r2.wait(eng, b)
            v = r2[:, 2 * i:2 * i + 2, :]
            s_r3.inc(eng.tensor_tensor(v, ps[:, 6 + i, :].rearrange("p (t h) -> p t h", t=2), v, ALU.add))
            if i:
                s_r3.wait(eng, b)

    def ln4(who, eng, b, chain):
        statistics(who, eng, b, "ln4", r2, chain)
        normalise(who, eng, b, "ln4", r2, x4, lambda e: (s_xstore.wait(e, b - 1), s_T["ln4"].wait(e, b - 1)))

    def ln4_T(who, eng, b):
        def free(e):
            s_r3.wait(e, b)
        transposes(who, eng, b, "ln4", x4, x4T, (6, 7), None, None, "dve", free)

    def affinity(who, eng, b, chain):
        if who == "pe":
            s_Te["ln4"].wait(eng, b)
            s_Td["ln4"].wait(eng, b)
            for t in range(NT):
                for kd in range(KD):
                    last = eng.matmul(ps[:, 6, t * NE:(t + 1) * NE], x4T[:, kd, t * P:(t + 1) * P], centT[:, kd, :],
                                      start=kd == 0, stop=kd == KD - 1)
            s_af.inc(last)
        elif who == "dve":
            s_af.wait(eng, b)
            s_rk.wait(eng, b - 1)
            d8 = g["desc8"].rearrange("p (t e) -> p t e", t=NT)
            s_afe.inc(eng.tensor_copy(aff[:, :, :], ps[:, 6, 0:NT * NE].rearrange("p (t e) -> p t e", t=NT)))
            s_afe.wait(eng, b)
            chain.link(eng.tensor_reduce(x4[:, :, H], aff[:, :, :], AX.X, ALU.max))
            chain.link(eng.tensor_tensor(ohf[:, :, :], aff[:, :, :],
                                         x4[:, :, H].unsqueeze(2).broadcast_to([P, NT, NE]), ALU.is_equal))
            chain.link(eng.tensor_tensor(ohf[:, :, :], ohf[:, :, :], d8, ALU.mult))
            chain.link(eng.tensor_reduce(amax2[:, :], ohf[:, :, :], AX.X, ALU.max))
            chain.link(eng.tensor_copy(cum[:, 0, :], cum[:, NT, :]))
            s_oh.inc(eng.tensor_tensor(oh[:, :, :], ohf[:, :, :],
                                       amax2[:, :].unsqueeze(2).broadcast_to([P, NT, NE]), ALU.is_equal))
            s_oh.wait(eng, b)
            for t in range(NT):
                chain.link(eng.tensor_tensor(cum[:, t + 1, :], cum[:, t, :], oh[:, t, :], ALU.add))
        elif who == "sp":
            s_oh.wait(eng, b)
            s_xstore.inc(eng.dma_start(xs_dram[bass.ds(b * S, S), :].rearrange("(t p) c -> p t c", p=P), x4[:, :, :]))

    def rank(who, eng, b, chain):
        if who == "pe":
            eng.wait_ge(sem_cf, b * PER_FFN + PER_FFN)
            eng.matmul(ps[:, 4, 0:NT * NE], triu_b[:, :], oh[:, :, :].rearrange("p t e -> p (t e)"),
                       start=True, stop=False)
            s_rk.inc(eng.matmul(ps[:, 4, 0:NT * NE], ones_b[:, :], cum[:, 0:NT, :].rearrange("p t e -> p (t e)"),
                                start=False, stop=True))
        elif who == "dve":
            s_rk.wait(eng, b)
            s_pos.wait(eng, b - 1)
            eb = g["ebase"].rearrange("p (t e) -> p t e", t=NT)
            chain.link(eng.tensor_tensor(posf[:, :, :], ps[:, 4, 0:NT * NE].rearrange("p (t e) -> p t e", t=NT), eb,
                                         ALU.add))
            chain.link(eng.tensor_tensor(posf[:, :, :], posf[:, :, :], oh[:, :, :], ALU.mult))
            chain.link(eng.tensor_reduce(pos1[:, :], posf[:, :, :], AX.X, ALU.add))
            for t in range(NT):
                s_scat[t].wait(eng, b - 1)
            eng.tensor_copy(posi[:, :], pos1[:, :])
            eng.tensor_copy(toki[:, :], tokf[:, :])
            s_pos.inc(eng.tensor_scalar(tokf[:, :], tokf[:, :], float(S), None, ALU.add))

    def scatter_ids(who, eng, b):
        if who == "pool":
            for t in range(NT):
                s_scat[t].wait(eng, b - 1)
            s_pos.wait(eng, b)
            eng.tensor_tensor(spare[:, 3:4], spare[:, 2:3], spare[:, 2:3], ALU.add)
            for t in range(NT):
                s_scat[t].inc(eng.indirect_dma_start(
                    out=table, out_offset=bass.IndirectOffsetOnAxis(ap=posi[:, t:t + 1], axis=0),
                    in_=toki[:, t:t + 1], in_offset=None))

    def iteration(who, eng, i, main, ffn, scatter, chains, next_x):
        cm, cf, cr = chains.get("m"), chains.get("f"), chains.get("r")
        f = i - 1
        if who == "dve":
            cm.begin(i)
            cf.begin(f)
            cr.begin(f)
        act_only, others = ("act", None) if who == "act" else (None, who)
        dve_only, not_dve = ("dve", None) if who == "dve" else (None, who)
        units = []
        if ffn:
            units = [lambda m=m: ffn1(who, eng, f, m) for m in range(FM)]
            units += [lambda t=t, h=h: ffn2(who, eng, f, t, h) for t in range(NT) for h in range(2)]

        def fill(count):
            for unit in units[:count]:
                unit()
            del units[:count]

        if main:
            if next_x:
                load_x(who, eng, i + 1)
            load_w1(who, eng, i)
        if ffn:
            ln3_T(who, eng, f)
        fill(3)
        if main:
            ln2(who, eng, i, cm)
            pre2(who, eng, i)
        if scatter:
            scatter_ids(who, eng, i - 2)
        if main:
            ln2_T(who, eng, i)
            fill(1)
            qkv(who, eng, i)
            fill(1)
            for n in range(STEPS + 1):
                if n < STEPS:
                    scores(who, eng, i, n)
                if n:
                    weigh(who, eng, i, n - 1)
                if n and n % 4 == 0:
                    group_out(act_only, eng, i, n // 4 - 1, cm)
                if n % 4 == 1 and n > 1 and n < STEPS:
                    group_out(others, eng, i, n // 4 - 1, cm)
                if n == 8 and next_x:
                    ln1(who, eng, i + 1, cm)
                    pre_a(who, eng, i + 1)
                if ffn and n == STEPS - NT:
                    assert not units
                    ln4(who, eng, f, cf)
                fill(1)
            if ffn:
                ln4_T(who, eng, f)
            group_out(others, eng, i, NG - 1, cm)
            if ffn:
                affinity(not_dve, eng, f, cf)
            ctx_T(who, eng, i)
            if ffn:
                affinity(dve_only, eng, f, cf)
            proj_o(who, eng, i)
            if next_x:
                ln1_T(who, eng, i + 1)
            ln3(who, eng, i, cm)
            residual2(who, eng, i)
            if next_x:
                pre_b(who, eng, i + 1)
                sf(who, eng, i + 1)
        elif ffn:
            fill(len(units))
            ln4(who, eng, f, cf)
            ln4_T(who, eng, f)
            affinity(who, eng, f, cf)
        if ffn:
            rank(who, eng, f, cr)
        if not main:
            scatter_ids(who, eng, f)
        if who == "dve":
            if main:
                if not next_x:
                    cm.k += 1
                cm.end()
            if ffn:
                cf.end()
                cr.end()

    def run(who, eng):
        chains = {}
        if who == "dve":
            chains = {"m": Chain(eng, sem_cm, PER_MAIN), "f": Chain(eng, sem_cf, PER_FFN),
                      "r": Chain(eng, sem_cr, PER_RANK)}
            chains["m"].begin(0)
        ln1(who, eng, 0, chains.get("m"))
        if who == "dve":
            chains["m"].ahead = 1
        pre_a(who, eng, 0)
        pre_b(who, eng, 0)
        ln1_T(who, eng, 0)
        sf(who, eng, 0)
        iteration(who, eng, 0, True, False, False, chains, True)
        if who == "pe":
            g["s_load_f"].wait(eng, 0)
        iteration(who, eng, 1, True, True, False, chains, True)
        with eng.Fori(2, NB - 1) as i:
            iteration(who, eng, i, True, True, True, chains, True)
        iteration(who, eng, NB - 1, True, True, True, chains, False)
        if who == "sp":
            load_w2(eng)
        iteration(who, eng, NB, False, True, True, chains, False)

    def load_w2(eng):
        s_wo.wait(eng, NB - 1)
        s_cTa.wait(eng, NB - 1)
        s_x2.wait(eng, NB - 1)
        s_r2.wait(eng, NB - 1)
        for e in range(NE):
            g["s_w2"].inc(eng.dma_start(g["arena"][:, e * FM * H:(e + 1) * FM * H], g["w2"][e * P:(e + 1) * P, :]))

    with nc.Block() as block:
        @block.sync
        def _(eng):
            load_x("sp", eng, 0)
            for sig, d, src in ((s_load, con[:, :], g["consts"]), (s_load, col[:, :], g["cols"]),
                                (s_load, sfT[:, :, :], g["sfw"]), (s_load, sfM[:, :, :], g["sfm"]),
                                (s_load, rowb[:, :, :], g["rows"]),
                                (s_load_a, wqT[:, :, :], g["wq"]), (s_load_a, wkT[:, :, :], g["wk"]),
                                (s_load_a, wvT[:, :, :], g["wv"]), (s_load_a, woT[:, :, :], g["wo"]),
                                (s_load_f, ff1T[:, :, :], g["ff1"]), (s_load_f, ff2T[:, :, :], g["ff2"]),
                                (s_load_f, centT[:, :, :], g["cent"]), (s_load_f, slc[:, :], g["slotc"])):
                sig.inc(eng.dma_start(d, src))
            s_fill.wait(eng, 0, 2)
            s_pad.inc(eng.dma_start(xs_dram[N_TOK:N_TOK + P, :], zrow[:, :]))
            run("sp", eng)
            s_xstore.wait(eng, NB - 1)
            s_pad.wait(eng, 0)

        @block.gpsimd
        def _(eng):
            eng.memset(spare[:, 2:4], 0.0)
            s_fill.inc(eng.memset(padid[:, :], N_TOK))
            s_fill.inc(eng.memset(zrow[:, :], 0.0))
            eng.memset(nhalf[:, :], -0.5)
            eng.memset(eps4[:, :], EPS)
            eng.memset(x4[:, :, H:XW], 0.0)
            eng.memset(ones_b[:, :], 1.0)
            eng.memset(vA[:, :, :, D + 1:32], 0.0)
            eng.memset(vA[:, :, :, D:D + 1], 1.0)
            s_fill.inc(eng.memset(cum[:, NT, :], 0.0))
            s_fill.wait(eng, 0)
            w = (NE + 1) * N_TOK // P // NT
            for t in range(NT):
                s_scat[t].inc(eng.dma_start(table.rearrange("(p c) o -> p (c o)", p=P)[:, t * w:(t + 1) * w],
                                            padid[:, t * w:(t + 1) * w]))
            s_load.wait(eng, 0)
            run("pool", eng)
            for t in range(NT):
                s_scat[t].wait(eng, NB - 1)

        @block.scalar
        def _(eng):
            s_load.wait(eng, 0)
            run("act", eng)

        @block.tensor
        def _(eng):
            s_load.wait(eng, 0)
            s_const.wait(eng, 0)
            s_fill.wait(eng, 0)
            run("pe", eng)
            s_cnt.inc(eng.matmul(ps[0:1, 0, 0:NE], ones_b[:, 0:1], cum[:, NT, :], start=True, stop=True))

        @block.vector
        def _(eng):
            eng.memset(spare[:, 0:2], 0.0)
            s_load.wait(eng, 0)
            s_fill.wait(eng, 0)
            eng.tensor_copy(triu_b[:, :], tri_u)
            s_pos.inc(eng.tensor_copy(tokf[:, :], g["tok0"]))
            s_const.inc(eng.tensor_tensor(sfT[:, :, :], sfT[:, :, :], sfM[:, :, :], ALU.mult))
            s_const.inc(eng.tensor_copy(ohf[:, :, :], g["desc8"].rearrange("p (t e) -> p t e", t=NT)))
            s_const.wait(eng, 0)
            run("dve", eng)

            s_load_f.wait(eng, 0)
            s_cnt.wait(eng, 0)
            ch = Chain(eng, sem_ct, 0)
            ch.begin(0)
            o = 0
            k128 = slc[:, o:o + NE * 32].rearrange("p (e k) -> p e k", e=NE)
            o += NE * 32
            le = slc[:, o:o + NE * NE].rearrange("p (e f) -> p e f", e=NE)
            o += NE * NE
            jj = slc[:, o:o + N_SLOT * NE].rearrange("p (j e) -> p j e", e=NE)
            o += N_SLOT * NE
            j1 = slc[:, o:o + N_SLOT]
            ch.link(eng.tensor_copy(cnt[:, :], ps[0:1, 0, 0:NE]))
            t8 = tmp[:, 0:NE * 32].rearrange("p (e k) -> p e k", e=NE)
            ch.link(eng.tensor_tensor(t8, cnt[:, :].unsqueeze(2).broadcast_to([1, NE, 32]), k128, ALU.is_gt))
            ch.link(eng.tensor_reduce(til[:, :], t8, AX.X, ALU.add))
            t8 = tmp[:, 0:NE * NE].rearrange("p (e f) -> p e f", e=NE)
            ch.link(eng.tensor_tensor(t8, til[:, :].unsqueeze(1).broadcast_to([1, NE, NE]), le, ALU.mult))
            ch.link(eng.tensor_reduce(end[:, :], t8, AX.X, ALU.add))
            ind = tmp[:, 0:N_SLOT * NE].rearrange("p (j e) -> p j e", e=NE)
            eb = end[:, :].unsqueeze(1).broadcast_to([1, N_SLOT, NE])
            tabf = g["tabf"]
            ch.link(eng.tensor_tensor(ind, eb, jj, ALU.is_le))
            ch.link(eng.tensor_reduce(tabf[:, 0, :], ind, AX.X, ALU.add))
            ch.link(eng.tensor_tensor(ind, ind, eb, ALU.mult))
            ch.link(eng.tensor_reduce(tabf[:, 1, :], ind, AX.X, ALU.max))
            ch.link(eng.tensor_tensor(tabf[:, 1, :], j1, tabf[:, 1, :], ALU.subtract))
            ch.link(eng.tensor_scalar(tabf[:, 1, :], tabf[:, 1, :], float(P), None, ALU.mult))
            ch.link(eng.scalar_tensor_tensor(out=tabf[:, 1, :], in0=tabf[:, 0, :], scalar=float(N_TOK),
                                             in1=tabf[:, 1, :], op0=ALU.mult, op1=ALU.add))
            ch.link(eng.tensor_scalar(tabf[:, 1, :], tabf[:, 1, :], float(NE * N_TOK), None, ALU.min))
            ch.link(eng.tensor_scalar(tabf[:, 2, :], tabf[:, 0, :], float(NE - 1), float(P), ALU.min, ALU.mult))
            ch.link(eng.tensor_scalar(tabf[:, 0, :], tabf[:, 0, :], float(NE - 1), float(KD * FF), ALU.min, ALU.mult))
            g["s_tab"].inc(eng.tensor_copy(g["tab"][:, :], tabf[:, :, :].rearrange("p a j -> p (a j)")))
            g["s_tab"].wait(eng, 0)


def phase_2(nc, stack, signal, sb_, ps, g):
    def sb(name, shape, dt=F32):
        return sb_(name, shape, dt, stack)

    ident, nhalf, tab, w1_sb = g["ident"], g["nhalf"], g["tab"], g["w1_sb"]
    xs_dram, table, epack, out = g["xs_dram"], g["table"], g["epack"], g["out"]
    spare, eps4 = g["spare"], g["eps4"]
    w2_sb = g["arena"]
    R = range(UN)
    ids = [sb(f"ids{u}", [P, 1], I32) for u in R]
    zero = sb("zero", [P, 1], I32)
    carry = sb("carry", [P, UN])
    ids2 = [sb(f"ids2{u}", [P, 1], I32) for u in R]
    ep = [sb(f"ep{u}", [P, EW]) for u in R]
    xg = [sb(f"xg{u}", [P, XW]) for u in R]
    xx = [sb(f"xx{u}", [P, H]) for u in R]
    ex = [sb(f"ex{u}", [P, 1]) for u in R]
    al = [sb(f"al{u}", [P, 1]) for u in R]
    xh = [sb(f"exh{u}", [P, H]) for u in R]
    xT = [sb(f"exT{u}", [P, KD, P]) for u in R]
    hs = [sb(f"hs{u}", [P, FF]) for u in R]
    hT = [sb(f"ehT{u}", [P, FM, P]) for u in R]
    rr = [sb(f"rr{u}", [P, H]) for u in R]
    oo = [sb(f"oo{u}", [P, H]) for u in R]
    st = [[sb(f"est{k}{u}", [P, 6]) for u in R] for k in range(2)]
    mv = [[sb(f"emv{k}{u}", [P, 2]) for u in R] for k in range(2)]
    rs = [[sb(f"ers{k}{u}", [P, 1]) for u in R] for k in range(2)]

    s_zero = signal("s_zero", 1)
    d_ids = [signal(f"d_ids{u}", 1, 16) for u in R]
    d_ep = [signal(f"d_ep{u}", 1, 16) for u in R]
    d_xg = [signal(f"d_xg{u}", 1, 16) for u in R]
    d_out = [signal(f"d_out{u}", 1, 16) for u in R]
    names = ("ids2", "ex", "xx", "e1", "al", "var0", "eps0", "rs0", "xh", "xT", "xTe", "l1", "l1a", "l1d", "hT",
             "hTa", "hTd", "l2", "y", "r", "var1", "eps1", "rs1", "o", "st0", "st1")
    sg = {n: signal(f"p_{n}", UN) for n in names}

    def wait(eng, n, m, u, ago=0):
        sg[n].wait(eng, m, u + 1 - ago)

    def wait_d(eng, d, m, u, ago=0):
        k = u - ago
        d[k % UN].wait(eng, m + k // UN)

    def at(m, u, ahead):
        k = u + ahead
        return m + k // UN, k % UN

    def fetch_ids(who, eng, m, u):
        if who == "sp":
            j = m * UN + u
            wait(eng, "ids2", m, u, UN)
            wait_d(eng, d_xg, m, u, UN)
            row = eng.value_load(tab[0:1, bass.ds(j + N_SLOT, 1)], min_val=0, max_val=NE * N_TOK)
            d_ids[u].inc(eng.dma_start(ids[u][:, :], table[bass.ds(row, P), :]))

    def fetch_ep(who, eng, m, u):
        if who == "sp":
            j = m * UN + u
            wait(eng, "y", m, u, UN)
            wait(eng, "hTa", m, u, UN)
            row = eng.value_load(tab[0:1, bass.ds(j + 2 * N_SLOT, 1)], min_val=0, max_val=(NE - 1) * P)
            d_ep[u].inc(eng.dma_start(ep[u][:, :], epack[bass.ds(row, P), :]))

    def gather(who, eng, m, u):
        if who == "pool":
            wait_d(eng, d_ids, m, u)
            wait(eng, "xh", m, u, UN)
            wait(eng, "xx", m, u, UN)
            eng.tensor_tensor(carry[:, u:u + 1], spare[:, 2:3], spare[:, 2:3], ALU.add)
            d_xg[u].inc(eng.indirect_dma_start(out=xg[u][:, :], out_offset=None, in_=xs_dram,
                                               in_offset=bass.IndirectOffsetOnAxis(ap=ids[u][:, :], axis=0)))

    def stats(who, eng, m, u, k, src, dst, done, ready):
        if who == "dve":
            sg[f"st{k}"].inc(eng.bn_stats(st[k][u][:, :], src))
            wait(eng, f"st{k}", m, u)
            eng.tensor_copy(spare[:, 1:2], spare[:, 0:1])
            sg[f"var{k}"].inc(eng.bn_aggr(mv[k][u][:, :], st[k][u][:, :]))
            wait(eng, f"rs{k}", m, u)
            ready(eng)
            sg[done].inc(eng.tensor_scalar(dst, src, mv[k][u][:, 0:1], rs[k][u][:, :], ALU.subtract, ALU.mult))
        elif who == "pool":
            wait(eng, f"var{k}", m, u)
            sg[f"eps{k}"].inc(eng.tensor_tensor(rs[k][u][:, :], mv[k][u][:, 1:2], eps4[:, 0:1], ALU.add))
            wait(eng, f"eps{k}", m, u)
            sg[f"rs{k}"].inc(eng.tensor_tensor(rs[k][u][:, :], rs[k][u][:, :], nhalf[:, 0:1], ALU.pow))

    def norm(who, eng, m, u):
        if who in ("dve", "act"):
            wait_d(eng, d_xg, m, u)
        stats(who, eng, m, u, 0, xg[u][:, 0:H], xh[u][:, :], "xh", lambda e: wait(e, "xT", m, u, UN))
        if who == "act":
            wait(eng, "al", m, u, UN)
            sg["ex"].inc(eng.activation(ex[u][:, :], xg[u][:, H:H + 1], ACT.Exp, scale=-1.0))
            wait(eng, "r", m, u, UN)
            sg["xx"].inc(eng.activation(xx[u][:, :], xg[u][:, 0:H], ACT.Copy, scale=2.0))
        elif who == "dve":
            wait(eng, "ex", m, u)
            sg["e1"].inc(eng.tensor_scalar(al[u][:, :], ex[u][:, :], 1.0, None, ALU.add))
            wait(eng, "e1", m, u)
            sg["al"].inc(eng.reciprocal(al[u][:, :], al[u][:, :]))

    def keep_ids(who, eng, m, u):
        if who == "pool":
            wait_d(eng, d_out, m, u, UN)
            sg["ids2"].inc(eng.tensor_tensor(ids2[u][:, :], ids[u][:, :], zero[:, :], ALU.add))

    def x_T(who, eng, m, u):
        if who == "pe":
            wait(eng, "xh", m, u)
            wait(eng, "xTe", m, u, 1)
            for kd in range(KD):
                last = eng.transpose(ps[:, 6, kd * P:(kd + 1) * P], xh[u][:, kd * P:(kd + 1) * P], ident)
            sg["xT"].inc(last)
        elif who == "act":
            wait(eng, "xT", m, u)
            wait_d(eng, d_ep, m, u)
            wait(eng, "l1", m, u, UN)
            for kd in range(KD):
                last = eng.activation(xT[u][:, kd, :], ps[:, 6, kd * P:(kd + 1) * P], ACT.Identity,
                                      bias=ep[u][:, E_B + kd:E_B + kd + 1], scale=ep[u][:, E_G + kd:E_G + kd + 1])
            sg["xTe"].inc(last)

    def layer1(who, eng, m, u):
        if who == "pe":
            col = eng.value_load(tab[0:1, bass.ds(m * UN + u, 1)], min_val=0, max_val=(NE - 1) * KD * FF)
            wait(eng, "xTe", m, u)
            wait(eng, "l1a", m, u, 1)
            wait(eng, "l1d", m, u, 1)
            for half in range(2):
                for kd in range(KD):
                    last = eng.matmul(ps[:, half, :], xT[u][:, kd, :],
                                      w1_sb[:, bass.ds(col + (kd * FF + half * 512), 512)],
                                      start=kd == 0, stop=kd == KD - 1)
            sg["l1"].inc(last)
        elif who == "act":
            wait(eng, "l1", m, u)
            wait(eng, "hT", m, u, UN)
            sg["l1a"].inc(eng.activation(hs[u][:, 0:512], ps[:, 0, :], ACT.Copy))
        elif who == "dve":
            wait(eng, "l1", m, u)
            wait(eng, "hT", m, u, UN)
            sg["l1d"].inc(eng.tensor_copy(hs[u][:, 512:1024], ps[:, 1, :]))

    def hidden_T(who, eng, m, u):
        if who == "pe":
            wait(eng, "l1a", m, u)
            wait(eng, "l1d", m, u)
            wait(eng, "hTa", m, u, 1)
            wait(eng, "hTd", m, u, 1)
            for f in range(FM):
                last = eng.transpose(ps[:, 2 + f // 4, (f % 4) * P:(f % 4 + 1) * P], hs[u][:, f * P:(f + 1) * P], ident)
            sg["hT"].inc(last)
        elif who in ("act", "dve"):
            wait(eng, "hT", m, u)
            wait(eng, "l2", m, u, UN)
            f0 = 0 if who == "act" else 4
            for f in range(f0, f0 + 4):
                o, i = hT[u][:, f, :], ps[:, 2 + f // 4, (f % 4) * P:(f % 4 + 1) * P]
                bias = ep[u][:, E_B1 + f:E_B1 + f + 1]
                if who == "act":
                    last = eng.activation(o, i, ACT.Relu, bias=bias)
                else:
                    last = eng.tensor_scalar(o, i, bias, 0.0, ALU.add, ALU.max)
            sg["hTa" if who == "act" else "hTd"].inc(last)

    def layer2(who, eng, m, u):
        if who == "pe":
            col = eng.value_load(tab[0:1, bass.ds(m * UN + u, 1)], min_val=0, max_val=(NE - 1) * FM * H)
            wait(eng, "hTa", m, u)
            wait(eng, "hTd", m, u)
            wait(eng, "y", m, u, 1)
            for f in range(FM):
                last = eng.matmul(ps[:, 4, 0:H], hT[u][:, f, :], w2_sb[:, bass.ds(col + f * H, H)],
                                  start=f == 0, stop=f == FM - 1)
            sg["l2"].inc(last)
        elif who == "dve":
            wait(eng, "l2", m, u)
            sg["y"].inc(eng.tensor_tensor(rr[u][:, :], ps[:, 4, 0:H], ep[u][:, E_B2:E_B2 + H], ALU.add))

    def finish(who, eng, m, u):
        if who == "dve":
            wait(eng, "xx", m, u)
            wait(eng, "al", m, u)
            wait(eng, "y", m, u)
            sg["r"].inc(eng.scalar_tensor_tensor(out=rr[u][:, :], in0=rr[u][:, :], scalar=al[u][:, :], in1=xx[u][:, :],
                                                 op0=ALU.mult, op1=ALU.add))
            wait(eng, "r", m, u)
        stats(who, eng, m, u, 1, rr[u][:, :], oo[u][:, :], "o", lambda e: wait_d(e, d_out, m, u, UN))

    def scatter(who, eng, m, u):
        if who == "pool":
            wait(eng, "o", m, u)
            eng.tensor_tensor(spare[:, 3:4], spare[:, 2:3], spare[:, 2:3], ALU.add)
            d_out[u].inc(eng.indirect_dma_start(out=out, out_offset=bass.IndirectOffsetOnAxis(ap=ids2[u][:, :], axis=0),
                                                in_=oo[u][:, :], in_offset=None, bounds_check=N_TOK - 1,
                                                oob_is_err=False))

    def slot(who, eng, m, u, first=False, last=False):
        left = UN - 1 - u if last else UN * N_SLOT
        if left >= 3:
            fetch_ids(who, eng, *at(m, u, 3))
        layer1(who, eng, m, u)
        if left >= 1:
            norm(who, eng, *at(m, u, 1))
        if not first or u > 1:
            scatter(who, eng, *at(m, u, -2))
        if left >= 3:
            gather(who, eng, *at(m, u, 3))
        if who == "pe" and (not first or u):
            layer2(who, eng, *at(m, u, -1))
        if left >= 1:
            x_T(who, eng, *at(m, u, 1))
        if who != "pe" and (not first or u):
            layer2(who, eng, *at(m, u, -1))
        hidden_T(who, eng, m, u)
        if not first or u:
            finish(who, eng, *at(m, u, -1))
        if left >= 2:
            fetch_ep(who, eng, *at(m, u, 2))
        if left >= 1:
            keep_ids(who, eng, *at(m, u, 1))

    def run(who, eng):
        M = N_SLOT // UN
        for u in range(3):
            fetch_ids(who, eng, 0, u)
        for u in range(2):
            fetch_ep(who, eng, 0, u)
        for u in range(3):
            gather(who, eng, 0, u)
        norm(who, eng, 0, 0)
        keep_ids(who, eng, 0, 0)
        x_T(who, eng, 0, 0)
        for u in R:
            slot(who, eng, 0, u, first=True)
        with eng.Fori(1, M - 1) as m:
            for u in R:
                slot(who, eng, m, u)
        for u in R:
            slot(who, eng, M - 1, u, last=True)
        layer2(who, eng, M - 1, UN - 1)
        scatter(who, eng, M - 1, UN - 2)
        finish(who, eng, M - 1, UN - 1)
        scatter(who, eng, M - 1, UN - 1)
        if who == "pool":
            for u in R:
                d_out[u].wait(eng, M - 1)

    with nc.Block() as block:
        @block.sync
        def _(eng):
            run("sp", eng)

        @block.gpsimd
        def _(eng):
            s_zero.inc(eng.memset(zero[:, :], 0))
            s_zero.wait(eng, 0)
            run("pool", eng)

        @block.scalar
        def _(eng):
            run("act", eng)

        @block.tensor
        def _(eng):
            g["s_w1"].wait(eng, 0)
            g["s_w2"].wait(eng, 0)
            run("pe", eng)

        @block.vector
        def _(eng):
            run("dve", eng)


def kernel(**inputs):
    import numpy as np
    import concourse.bacc as bacc
    from concourse.bass_utils import run_bass_kernel_spmd

    a = {k: np.asarray(v) for k, v in inputs.items()}

    def by_rows(w):
        return np.ascontiguousarray(w.T.reshape(-1, P, w.shape[0]).transpose(1, 0, 2))

    def column(v):
        return v.reshape(-1, P).T

    f32 = np.float32
    c = "L0_attn_"
    half = (np.arange(P) // D % 2)[:, None]
    scale = f32(D ** -0.5)
    cols = np.concatenate([column(a[c + n]) for n in ("g1", "b1", "g2", "b2", "g3", "b3", "bq", "bk", "ff1_b")]
                          + [(half == 0) * scale, (half == 1) * scale], axis=1).astype(f32)
    rows = np.stack([np.broadcast_to(a[c + n], (P, H)) for n in ("sf_b", "bo", "ff2_b", "bv")], axis=1)
    i = np.arange(P)
    e = np.arange(NE)
    consts = np.concatenate([
        np.eye(P), i[:, None] < i[None, :], i[:, None] <= np.arange(S)[None, :],
        np.broadcast_to(np.tile(NE - e, NT), (P, NT * NE)), np.broadcast_to(np.tile(e * N_TOK, NT), (P, NT * NE)),
        i[:, None] + P * np.arange(NT)[None, :]], axis=1).astype(f32)
    slotc = np.concatenate([np.tile(P * np.arange(32), NE), np.tril(np.ones((NE, NE))).ravel(),
                            np.repeat(np.arange(N_SLOT), NE), np.arange(N_SLOT)])[None, :].astype(f32)
    f = "L0_ffn_"
    w1 = np.concatenate([by_rows(w).reshape(P, -1) for w in a[f + "w1"]], axis=0)
    w2 = np.concatenate([by_rows(w).reshape(P, -1) for w in a[f + "w2"]], axis=0)
    epack = np.concatenate([np.concatenate([column(a[f + "ln_g"][k]), column(a[f + "ln_b"][k]),
                                            column(a[f + "b1"][k]), np.broadcast_to(a[f + "b2"][k], (P, H))], axis=1)
                            for k in range(NE)], axis=0)
    arrays = dict(x=a[c + "x"].reshape(N_TOK, H), sfw=by_rows(a[c + "sf_w"]), sfm=by_rows(a[c + "mask"]),
                  wq=by_rows(a[c + "wq"]), wk=by_rows(a[c + "wk"]), wv=by_rows(a[c + "wv"]), wo=by_rows(a[c + "wo"]),
                  ff1=by_rows(a[c + "ff1_w"]), ff2=by_rows(a[c + "ff2_w"]), cent=by_rows(a[f + "centroids"]),
                  rows=rows, cols=cols, consts=consts, slotc=slotc, w1=w1, w2=w2, epack=epack)
    nc = bacc.Bacc("TRN2", target_bir_lowering=False, num_devices=1)
    args, feed = [], {}
    for name, v in arrays.items():
        v = np.ascontiguousarray(v)
        feed[f"in_{name}"] = v
        args.append(nc.dram_tensor(f"in_{name}", v.shape, mybir.dt.from_np(v.dtype), kind="ExternalInput").ap())
    out = nc.dram_tensor("out_y", (N_TOK, H), F32, kind="ExternalOutput").ap()
    build(nc, *args, out)
    r = run_bass_kernel_spmd(nc, [feed], core_ids=[0])
    return r.results[0]["out_y"].reshape(NB, S, H)
```

```python
from contextlib import ExitStack

import concourse.bass as bass
from concourse import mybir

ALU = mybir.AluOpType
ACT = mybir.ActivationFunctionType
AX = mybir.AxisListType
F32 = mybir.dt.float32
BF16 = mybir.dt.bfloat16
I32 = mybir.dt.int32
U32 = mybir.dt.uint32

P = 128
NB, S, H = 8, 512, 256
NT = S // P
KD = H // P
NH, D = 16, 16
FF = 4 * H
FM = FF // P
NG = 4
NE = 8
N_TOK = NB * S
N_SLOT = (N_TOK + NE * (P - 1)) // P
XW = H + 4
EPS = 1e-5
UN = 3
assert N_SLOT % UN == 0

C_G1, C_B1, C_G2, C_B2, C_G3, C_B3, C_BQ, C_BK, C_F1B, C_ME, C_MO = 0, 2, 4, 6, 8, 10, 12, 14, 16, 24, 25
NCOL = 26
NCON = 2 * P + S + 2 * NT * NE + NT
NSLC = NE * 32 + NE * NE + N_SLOT * NE + N_SLOT
E_G, E_B, E_B1, E_B2 = 0, 2, 4, 12
EW = 12 + H


class Signal:

    def __init__(self, sem, per, step=1, ahead=0):
        self.sem, self.per, self.step, self.ahead = sem, per, step, ahead

    def inc(self, ins):
        return ins.then_inc(self.sem, self.step)

    def wait(self, eng, rnd, k=None):
        k = self.per if k is None else k
        value = rnd * (self.per * self.step) + (k + self.ahead) * self.step
        if isinstance(value, int) and value <= 0:
            return
        eng.wait_ge(self.sem, value)


class Chain:

    def __init__(self, eng, sem, per, ahead=0):
        self.eng, self.sem, self.per, self.k, self.ahead = eng, sem, per, 0, ahead

    def begin(self, rnd):
        self.rnd, self.k = rnd, self.ahead

    def link(self, ins):
        self.k += 1
        ins.then_inc(self.sem, 1)
        self.eng.wait_ge(self.sem, self.rnd * self.per + self.k)

    def end(self):
        assert self.k == self.per + self.ahead, (self.k, self.per)


def build(nc, x, sfw, sfm, wq, wk, wv, wo, ff1, ff2, cent, rows, cols, consts, slotc, w1, w2, epack, out):
    xs_dram = nc.dram_tensor("token_store", (N_TOK + P, XW), F32, kind="Internal").ap()
    table = nc.dram_tensor("slot_table", ((NE + 1) * N_TOK, 1), I32, kind="Internal").ap()
    ctx = ExitStack()
    with ctx:
        def sb(name, shape, dt=F32, stack=ctx):
            return stack.enter_context(nc.sbuf_tensor(name, shape, dt))

        def signal(name, per, step=1, ahead=0):
            return Signal(ctx.enter_context(nc.semaphore(name)), per, step, ahead)

        ps = ctx.enter_context(nc.psum_tensor("ps", [P, 8, 512], F32))

        w1_sb = sb("w1_sb", [P, NE * KD * FF])
        arena = sb("arena", [P, NE * FM * H])
        con = sb("con", [P, NCON])
        ident = con[:, 0:P]
        tri_u = con[:, P:2 * P]
        causal = con[:, 2 * P:2 * P + S]
        desc8 = con[:, 2 * P + S:2 * P + S + 32]
        ebase = con[:, 2 * P + S + 32:2 * P + S + 64]
        tok0 = con[:, 2 * P + S + 64:2 * P + S + 68]
        slc = sb("slc", [1, NSLC])
        nhalf = sb("nhalf", [P, NT])
        eps4 = sb("eps4", [P, NT])
        tab = sb("tab", [1, 3 * N_SLOT], I32)
        tabf = sb("tabf", [1, 3, N_SLOT])

        spare = sb("spare", [P, 4])
        s_load = signal("s_load", 5, 16)
        s_load_a = signal("s_load_a", 4, 16)
        s_load_f = signal("s_load_f", 4, 16)
        s_w1 = signal("s_w1", NE, 16)
        s_w2 = signal("s_w2", NE, 16)
        s_xstore = signal("s_xstore", 1, 16)
        s_scat = [signal(f"s_scat{t}", 1, 16, ahead=1) for t in range(NT)]
        s_pad = signal("s_pad", 1, 16)
        s_tab = signal("s_tab", 1)

        env = dict(ctx=ctx, w1_sb=w1_sb, con=con, ident=ident, tri_u=tri_u, causal=causal, desc8=desc8, ebase=ebase,
                   tok0=tok0, slc=slc, nhalf=nhalf, eps4=eps4, tab=tab, tabf=tabf, s_load=s_load, s_load_a=s_load_a,
                   s_load_f=s_load_f, arena=arena, spare=spare, s_w1=s_w1, s_w2=s_w2, s_xstore=s_xstore,
                   s_scat=s_scat, s_pad=s_pad, s_tab=s_tab, xs_dram=xs_dram, table=table, x=x, sfw=sfw, sfm=sfm,
                   wq=wq, wk=wk, wv=wv, wo=wo, ff1=ff1, ff2=ff2, cent=cent, rows=rows, cols=cols, consts=consts,
                   slotc=slotc, w1=w1, w2=w2, epack=epack, out=out)
        phase1 = ExitStack()
        with phase1:
            phase_1(nc, phase1, signal, sb, ps, env)
        phase2 = ExitStack()
        with phase2:
            phase_2(nc, phase2, signal, sb, ps, env)


def phase_1(nc, stack, signal, sb_, ps, g):
    def sb(name, shape, dt=F32):
        return sb_(name, shape, dt, stack)

    con, slc, nhalf, ident, tri_u, causal = g["con"], g["slc"], g["nhalf"], g["ident"], g["tri_u"], g["causal"]
    x, xs_dram, table = g["x"], g["xs_dram"], g["table"]
    s_xstore, s_scat, s_pad = g["s_xstore"], g["s_scat"], g["s_pad"]

    sfT = sb("sfT", [P, KD, H])
    wqT = sb("wqT", [P, KD, H])
    wkT = sb("wkT", [P, KD, H])
    wvT = sb("wvT", [P, KD, H])
    woT = sb("woT", [P, KD, H])
    ff1T = sb("ff1T", [P, KD, FF])
    ff2T = sb("ff2T", [P, FM, H])
    centT = sb("centT", [P, KD, NE])
    rowb = sb("rowb", [P, 4, H])
    col = sb("col", [P, NCOL])
    bkm = sb("bkm", [P, 2])
    triu_b = sb("triu_b", [P, P], BF16)
    ones_b = sb("ones_b", [P, P], BF16)
    padid = sb("padid", [P, (NE + 1) * N_TOK // P], I32)
    zrow = sb("zrow", [P, XW])

    parts, at = {}, 0
    for name, size in (("xin", NT * H), ("xkf", NT * H), ("x1", NT * H), ("xh", NT * H), ("xT", KD * S), ("qT", KD * S),
                       ("kT", KD * 2 * S), ("vA", NT * NH * 32), ("att", 2 * 4 * S), ("num", S), ("ctxt", NT * H)):
        parts[name] = g["arena"][:, at:at + size]
        at += size
    assert at <= NE * FM * H

    def tiles(name):
        return parts[name].rearrange("p (t h) -> p t h", h=H)

    xin = tiles("xin")
    xkf = tiles("xkf")
    x1 = tiles("x1")
    xh = tiles("xh")
    ctxt = tiles("ctxt")
    xT = parts["xT"].rearrange("p (k s) -> p k s", k=KD)
    qT = parts["qT"].rearrange("p (k s) -> p k s", k=KD)
    kT = parts["kT"].rearrange("p (k g s) -> p k g s", k=KD, g=2)
    vA = parts["vA"].rearrange("p (t h c) -> p t h c", t=NT, h=NH)
    att = parts["att"].rearrange("p (b f s) -> p b f s", b=2, f=4)
    num = parts["num"]
    x2 = sb("x2", [P, NT, H])
    den = sb("den", [P, NT, 4])
    rden = sb("rden", [P, NT, 4])
    xh3 = sb("xh3", [P, NT, H])
    xT3 = sb("xT3", [P, KD, S])
    hT = sb("hT", [P, FM, S])
    ctxT = hT[:, 0:KD, :]
    sfM = hT[:, 0, :].rearrange("p (k h) -> p k h", k=KD)
    r2 = sb("r2", [P, NT, H])
    x4 = sb("x4", [P, NT, XW])
    x4T = xT3
    aff = sb("aff", [P, NT, NE])
    ohf = sb("ohf", [P, NT, NE])
    amax2 = sb("amax2", [P, NT])
    oh = sb("oh", [P, NT, NE], BF16)
    cum = sb("cum", [P, NT + 1, NE], BF16)
    posf = sb("posf", [P, NT, NE])
    pos1 = sb("pos1", [P, NT])
    posi = sb("posi", [P, NT], U32)
    tokf = sb("tokf", [P, NT])
    toki = sb("toki", [P, NT], I32)
    tmp = sb("tmp", [1, N_SLOT * NE])
    cnt, til, end = sb("cnt", [1, NE]), sb("til", [1, NE]), sb("end", [1, NE])
    stats = {w: sb(f"st_{w}", [P, NT, 6]) for w in ("ln1", "ln2", "ln3", "ln4")}
    mv = {w: sb(f"mv_{w}", [P, NT, 2]) for w in stats}
    rstd = {w: sb(f"rs_{w}", [P, NT]) for w in stats}

    s_load, s_load_a, s_load_f = g["s_load"], g["s_load_a"], g["s_load_f"]
    spare, eps4 = g["spare"], g["eps4"]
    s_const = signal("s_const", 3)
    s_fill = signal("s_fill", 3)
    s_x = signal("s_x", 1, 16)
    s_pa = signal("s_pa", 1)
    s_pb = signal("s_pb", 1)
    s_var = {w: signal(f"s_var_{w}", 1) for w in stats}
    s_eps = {w: signal(f"s_eps_{w}", 1) for w in stats}
    s_rs = {w: signal(f"s_rs_{w}", 1) for w in stats}
    s_xh = {w: signal(f"s_xh_{w}", 1) for w in stats}
    s_T = {w: signal(f"s_T_{w}", 2) for w in stats}
    s_Te = {w: signal(f"s_Te_{w}", 1) for w in stats}
    s_Td = {w: signal(f"s_Td_{w}", 1) for w in stats}
    s_sf = signal("s_sf", 2)
    s_x1 = signal("s_x1", 2)
    s_xb2 = signal("s_xb2", 1)
    s_q = signal("s_q", 2)
    s_k = signal("s_k", 2)
    s_v = signal("s_v", 2)
    s_qe = signal("s_qe", 2)
    s_ke = signal("s_ke", 1)
    s_ka = signal("s_ka", 1)
    s_ve = signal("s_ve", 2)
    STEPS = NG * NT
    s_s = signal("s_s", 2 * STEPS)
    s_sa = signal("s_sa", STEPS)
    s_sm = signal("s_sm", STEPS)
    s_sd = signal("s_sd", STEPS)
    s_av = signal("s_av", STEPS)
    s_num = signal("s_num", NG)
    s_ct = signal("s_ct", NG)
    s_ctx = signal("s_ctx", NG)
    s_cT = signal("s_cT", 2)
    s_cTa = signal("s_cTa", 2)
    s_wo = signal("s_wo", 2)
    s_x2 = signal("s_x2", 2)
    s_r2 = signal("s_r2", 1)
    s_f1 = signal("s_f1", FM)
    s_f1e = signal("s_f1e", FM)
    s_f2 = signal("s_f2", 2)
    s_r3 = signal("s_r3", 2)
    s_af = signal("s_af", 1)
    s_afe = signal("s_afe", 1)
    s_oh = signal("s_oh", 1)
    s_rk = signal("s_rk", 1)
    s_pos = signal("s_pos", 1, ahead=1)
    s_cnt = signal("s_cnt", 1)
    sem_cm = g["ctx"].enter_context(nc.semaphore("chain_main"))
    sem_cf = g["ctx"].enter_context(nc.semaphore("chain_ffn"))
    sem_cr = g["ctx"].enter_context(nc.semaphore("chain_route"))
    sem_ct = g["ctx"].enter_context(nc.semaphore("chain_table"))
    sem_cp = g["ctx"].enter_context(nc.semaphore("chain_pool"))

    WARM, WARM_N = 4, 512
    LAST_FILL = 12
    PER_MAIN = 3 + 2 * NG
    PER_FFN = 6 + NT
    PER_RANK = 3

    last_stats = {}

    def row(k):
        return rowb[:, k, :].unsqueeze(1).broadcast_to([P, NT, H])

    def row_stats(eng, w, src, half):
        for t in (2 * half, 2 * half + 1):
            last = eng.bn_stats(stats[w][:, t, :], src[:, t, 0:H])
        return last

    def add_product(who, eng, b, w, ready, bank, dst, done, chain):
        for i in range(2):
            ready.wait(eng, b, i + 1)
            v = dst[:, 2 * i:2 * i + 2, :]
            done.inc(eng.tensor_tensor(v, ps[:, bank + i, :].rearrange("p (t h) -> p t h", t=2), v, ALU.add))
            done.wait(eng, b, i + 1)
            last = row_stats(eng, w, dst, i)
        return last

    def statistics(who, eng, b, w, last, chain):
        if who == "dve":
            chain.link(last)
            eng.tensor_copy(spare[:, 1:2], spare[:, 0:1])
            for t in range(NT):
                last = eng.bn_aggr(mv[w][:, t, :], stats[w][:, t, :])
            s_var[w].inc(last)
        elif who == "pool":
            s_var[w].wait(eng, b)
            s_eps[w].inc(eng.tensor_tensor(rstd[w][:, :], mv[w][:, :, 1], eps4[:, 0:NT], ALU.add))
            s_eps[w].wait(eng, b)
            s_rs[w].inc(eng.tensor_tensor(rstd[w][:, :], rstd[w][:, :], nhalf[:, 0:NT], ALU.pow))

    def normalise(who, eng, b, w, src, dst, ready):
        if who == "dve":
            ready(eng)
            s_rs[w].wait(eng, b)
            for t in range(NT):
                last = eng.tensor_scalar(dst[:, t, 0:H], src[:, t, 0:H], mv[w][:, t, 0:1], rstd[w][:, t:t + 1],
                                         ALU.subtract, ALU.mult)
            s_xh[w].inc(last)

    def transposes(who, eng, b, w, src, dst, banks, gc=None, bc=None, second="act", free=None):
        if who == "pe":
            s_xh[w].wait(eng, b)
            if free:
                free(eng)
            for kd in range(KD):
                for t in range(NT):
                    last = eng.transpose(ps[:, banks[kd], t * P:(t + 1) * P], src[:, t, kd * P:(kd + 1) * P], ident)
                s_T[w].inc(last)
            return
        for kd, owner, sig in ((0, "act", s_Te[w]), (1, second, s_Td[w])):
            if who != owner:
                continue
            s_T[w].wait(eng, b, kd + 1)
            o, i = dst[:, kd, :], ps[:, banks[kd], :]
            if owner == "act":
                if gc is None:
                    sig.inc(eng.activation(o, i, ACT.Copy))
                else:
                    sig.inc(eng.activation(o, i, ACT.Identity, bias=col[:, bc + kd:bc + kd + 1],
                                           scale=col[:, gc + kd:gc + kd + 1]))
            elif gc is None:
                sig.inc(eng.tensor_copy(o, i))
            else:
                sig.inc(eng.tensor_scalar(o, i, col[:, gc + kd:gc + kd + 1], col[:, bc + kd:bc + kd + 1],
                                          ALU.mult, ALU.add))

    def load_x(who, eng, b):
        if who == "sp":
            s_pa.wait(eng, b - 1)
            s_pb.wait(eng, b - 1)
            s_xh["ln1"].wait(eng, b - 1)
            s_x.inc(eng.dma_start(xin[:, :, :], x[bass.ds(b * S, S), :].rearrange("(t p) h -> p t h", p=P)))

    def load_w1(who, eng, b):
        if who == "sp":
            g["s_w1"].inc(eng.dma_start(g["w1_sb"][:, bass.ds(b * (KD * FF), KD * FF)],
                                        g["w1"][bass.ds(b * P, P), :]))

    def pre_a(who, eng, b):
        if who == "pool":
            s_x.wait(eng, b)
            s_xh["ln2"].wait(eng, b - 1)
            s_pa.inc(eng.tensor_tensor(x1[:, :, :], xin[:, :, :], row(0), ALU.add))

    def pre_b(who, eng, b):
        if who == "pool":
            s_r2.wait(eng, b - 1)
            s_pb.inc(eng.tensor_tensor(xkf[:, :, :], xin[:, :, :], row(2), ALU.add))

    def ln1(who, eng, b, chain, between=None):
        last = None
        if who == "dve":
            s_x.wait(eng, b)
            row_stats(eng, "ln1", xin, 0)
            last = row_stats(eng, "ln1", xin, 1)
        statistics(who, eng, b, "ln1", last, chain)
        if between:
            between()
        normalise(who, eng, b, "ln1", xin, xh, lambda e: s_T["ln2"].wait(e, b - 1))

    def ln1_T(who, eng, b):
        def free(e):
            s_sa.wait(e, b - 1)
        if who == "act":
            s_v.wait(eng, b - 1)
        transposes(who, eng, b, "ln1", xh, xT, (0, 1), C_G1, C_B1, "act", free)

    def sf(who, eng, b, chain):
        if who == "pe":
            s_Te["ln1"].wait(eng, b)
            s_Td["ln1"].wait(eng, b)
            s_sd.wait(eng, b - 1)
            for t in range(NT):
                for kd in range(KD):
                    last = eng.matmul(ps[:, 2 + t // 2, (t % 2) * H:(t % 2) * H + H], xT[:, kd, t * P:(t + 1) * P],
                                      sfT[:, kd, :], start=kd == 0, stop=kd == KD - 1)
                if t % 2:
                    s_sf.inc(last)
        elif who == "dve":
            s_pa.wait(eng, b)
            return add_product(who, eng, b, "ln2", s_sf, 2, x1, s_x1, chain)

    def pre2(who, eng, b):
        if who == "pool":
            s_x1.wait(eng, b)
            s_xh["ln3"].wait(eng, b - 1)
            s_r2.wait(eng, b - 1)
            s_xb2.inc(eng.tensor_tensor(x2[:, :, :], x1[:, :, :], row(1), ALU.add))

    def ln2(who, eng, b, last, chain):
        statistics(who, eng, b, "ln2", last, chain)
        normalise(who, eng, b, "ln2", x1, xh, lambda e: s_T["ln1"].wait(e, b))

    def ln2_T(who, eng, b):
        def free(e):
            s_cTa.wait(e, b - 1)
        if who in ("act", "dve"):
            s_sf.wait(eng, b)
        transposes(who, eng, b, "ln2", xh, xT, (0, 1), C_G2, C_B2, "dve", free)

    def queries_keys(who, eng, b):
        if who == "pe":
            if isinstance(b, int) and b == 0:
                s_load_a.wait(eng, 0)
            s_Te["ln2"].wait(eng, b)
            s_Td["ln2"].wait(eng, b)
            for w, b0, sig in ((wqT, 2, s_q), (wkT, 4, s_k)):
                if b0 == 2:
                    s_x1.wait(eng, b)
                else:
                    s_x2.wait(eng, b - 1)
                for m in range(KD):
                    for kd in range(KD):
                        last = eng.matmul(ps[:, b0 + m, :], w[:, kd, m * P:(m + 1) * P], xT[:, kd, :],
                                          start=kd == 0, stop=kd == KD - 1)
                    sig.inc(last)
        elif who == "act":
            s_s.wait(eng, b - 1)
            for m in range(KD):
                s_q.wait(eng, b, m + 1)
                s_qe.inc(eng.activation(qT[:, m, :], ps[:, 2 + m, :], ACT.Identity, bias=col[:, C_BQ + m:C_BQ + m + 1]))
            s_k.wait(eng, b, 1)
            for par, mask in ((0, C_ME), (1, C_MO)):
                last = eng.activation(kT[:, 0, par, :], ps[:, 4, :], ACT.Identity, bias=bkm[:, par:par + 1],
                                      scale=col[:, mask:mask + 1])
            s_ka.inc(last)
        elif who == "dve":
            s_s.wait(eng, b - 1)
            s_k.wait(eng, b, 2)
            for par, mask in ((0, C_ME), (1, C_MO)):
                last = eng.tensor_scalar(kT[:, 1, par, :], ps[:, 5, :], col[:, C_BK + 1:C_BK + 2],
                                         col[:, mask:mask + 1], ALU.add, ALU.mult)
            s_ke.inc(last)

    def values(who, eng, b):
        if who == "pe":
            for t in range(NT):
                if t == 2:
                    s_pos.wait(eng, b - 2)
                for kd in range(KD):
                    last = eng.matmul(ps[:, t // 2, (t % 2) * H:(t % 2) * H + H], xT[:, kd, t * P:(t + 1) * P],
                                      wvT[:, kd, :], start=kd == 0, stop=kd == KD - 1)
                if t % 2:
                    s_v.inc(last)
        elif who == "dve":
            s_av.wait(eng, b - 1)
            for i in range(2):
                s_v.wait(eng, b, i + 1)
                for j in range(2):
                    last = eng.tensor_tensor(vA[:, 2 * i + j, :, 0:D],
                                             ps[:, i, j * H:(j + 1) * H].rearrange("p (h d) -> p h d", h=NH),
                                             rowb[:, 3, :].rearrange("p (h d) -> p h d", h=NH), ALU.add)
                s_ve.inc(last)

    def scores(who, eng, b, n, between=None):
        gt, gp, kt = n // 8, (n // 4) % 2, n % 4
        q0, w = kt * P, S - kt * P
        buf = n % 2
        if who == "pe":
            if n == 0:
                s_qe.wait(eng, b)
                s_ka.wait(eng, b)
                s_ke.wait(eng, b)
                s_ve.wait(eng, b)
            for s in range(4):
                if n and s == 0:
                    s_sa.wait(eng, b, n)
                elif n and s == 2:
                    s_sd.wait(eng, b, n)
                r = slice(32 * s, 32 * s + 32)
                last = eng.matmul(ps[:, s, q0:S], kT[r, gt, gp, q0:q0 + P], qT[r, gt, q0:S], start=True, stop=True)
                if s % 2:
                    s_s.inc(last)
                if s == 1 and between:
                    between()
        elif who == "act":
            s_s.wait(eng, b, 2 * n + 1)
            s_av.wait(eng, b, n - 1)
            s_sa.inc(eng.activation(att[:, buf, 0:2, q0:S], ps[:, 0:2, q0:S], ACT.Relu))
        elif who == "pool":
            s_sa.wait(eng, b, n + 1)
            v = att[:, buf, 0:2, q0:q0 + P]
            s_sm.inc(eng.tensor_tensor(v, v, causal[:, 0:P].unsqueeze(1).broadcast_to([P, 2, P]), ALU.mult))
        elif who == "dve":
            s_s.wait(eng, b, 2 * n + 2)
            s_av.wait(eng, b, n - 1)
            for s in (2, 3):
                last = eng.scalar_tensor_tensor(out=att[:, buf, s, q0:S], in0=ps[:, s, q0:S], scalar=0.0,
                                                in1=causal[:, 0:w], op0=ALU.max, op1=ALU.mult)
            s_sd.inc(last)

    def weigh(who, eng, b, n):
        if who != "pe":
            return
        gt, gp, kt = n // 8, (n // 4) % 2, n % 4
        q0, buf = kt * P, n % 2
        if n == 0:
            s_ka.wait(eng, b)
        elif kt == 0:
            s_num.wait(eng, b, n // 4)
        for s in range(4):
            if s == 0:
                s_sm.wait(eng, b, n + 1)
            elif s == 2:
                s_sd.wait(eng, b, n + 1)
            head = 8 * gt + 2 * s + gp
            last = eng.matmul(ps[32 * s:32 * s + 32, 4, q0:S], vA[:, kt, head, :], att[:, buf, s, q0:S],
                              start=kt == 0, stop=kt == NT - 1)
        s_av.inc(last)

    def group_out(who, eng, b, grp, chain):
        gt, gp = grp // 2, grp % 2
        if who == "act":
            s_av.wait(eng, b, 4 * grp + 4)
            if grp == 0:
                s_ct.wait(eng, b - 1)
            else:
                s_ct.wait(eng, b, grp)
            s_num.inc(eng.activation(num[:, :], ps[:, 4, :], ACT.Copy))
        elif who == "pe":
            s_num.wait(eng, b, grp + 1)
            if grp:
                s_ctx.wait(eng, b, grp)
            for t in range(NT):
                last = eng.transpose(ps[:, 5, t * P:(t + 1) * P], num[:, t * P:(t + 1) * P], ident)
            s_ct.inc(last)
        elif who == "dve":
            s_ct.wait(eng, b, grp + 1)
            v = ps[:, 5, :].rearrange("p (t s c) -> p t s c", t=NT, s=4)
            chain.link(eng.tensor_scalar(den[:, :, :], v[:, :, :, D], 1e-9, None, ALU.add))
            chain.link(eng.reciprocal(rden[:, :, :], den[:, :, :]))
            if grp == 0:
                s_cT.wait(eng, b - 1)
            o = ctxt[:, :, :].rearrange("p t (g s q d) -> p g q t s d", g=2, s=4, q=2)
            for t in range(NT):
                last = eng.tensor_tensor(o[:, gt, gp, t], v[:, t, :, 0:D],
                                         rden[:, t, :].unsqueeze(2).broadcast_to([P, 4, D]), ALU.mult)
            s_ctx.inc(last)

    def ctx_T(who, eng, b, ffn, next_x):
        if who == "pe":
            s_ctx.wait(eng, b)
            if next_x:
                s_Te["ln1"].wait(eng, b + 1)
                s_Td["ln1"].wait(eng, b + 1)
            else:
                s_sa.wait(eng, b)
            for kd in range(KD):
                for t in range(NT):
                    last = eng.transpose(ps[:, kd, t * P:(t + 1) * P], ctxt[:, t, kd * P:(kd + 1) * P], ident)
                s_cT.inc(last)
        elif who == "act":
            if ffn:
                s_f2.wait(eng, b - 1)
            else:
                s_const.wait(eng, 0)
            for kd in range(KD):
                s_cT.wait(eng, b, kd + 1)
                s_cTa.inc(eng.activation(ctxT[:, kd, :], ps[:, kd, :], ACT.Copy))

    def proj_o(who, eng, b, tiles):
        if who == "pe":
            if tiles[0] == 0:
                s_cTa.wait(eng, b)
            for t in tiles:
                for kd in range(KD):
                    last = eng.matmul(ps[:, 4 + t // 2, (t % 2) * H:(t % 2) * H + H], ctxT[:, kd, t * P:(t + 1) * P],
                                      woT[:, kd, :], start=kd == 0, stop=kd == KD - 1)
                if t % 2:
                    s_wo.inc(last)

    def add_o(who, eng, b, chain):
        if who == "dve":
            s_xb2.wait(eng, b)
            return add_product(who, eng, b, "ln3", s_wo, 4, x2, s_x2, chain)

    def residual2(who, eng, b):
        if who == "pool":
            s_x2.wait(eng, b)
            s_xh["ln4"].wait(eng, b - 1)
            s_r2.inc(eng.tensor_tensor(r2[:, :, :], xkf[:, :, :], x2[:, :, :], ALU.add))

    def ln3(who, eng, b, last, chain, between):
        statistics(who, eng, b, "ln3", last, chain)
        between()
        normalise(who, eng, b, "ln3", x2, xh3, lambda e: s_T["ln3"].wait(e, b - 1))

    def ln3_T(who, eng, b):
        def free(e):
            s_afe.wait(e, b - 1)
            s_Td["ln4"].wait(e, b - 1)
        if who in ("act", "dve"):
            s_af.wait(eng, b - 1)
        transposes(who, eng, b, "ln3", xh3, xT3, (6, 7), C_G3, C_B3, "act", free)

    def ffn1(who, eng, b, m):
        if who == "pe":
            if m == 0:
                s_Te["ln3"].wait(eng, b)
                s_Td["ln3"].wait(eng, b)
            if m >= 2:
                s_f1e.wait(eng, b, m - 1)
            for kd in range(KD):
                last = eng.matmul(ps[:, 6 + m % 2, :], ff1T[:, kd, m * P:(m + 1) * P], xT3[:, kd, :],
                                  start=kd == 0, stop=kd == KD - 1)
            s_f1.inc(last)
        elif who == "act":
            s_f1.wait(eng, b, m + 1)
            if m == 0:
                s_f2.wait(eng, b - 1)
                s_wo.wait(eng, b)
            s_f1e.inc(eng.activation(hT[:, m, :], ps[:, 6 + m % 2, :], ACT.Relu,
                                     bias=col[:, C_F1B + m:C_F1B + m + 1]))

    def ffn2(who, eng, b, t, half):
        if who == "pe":
            if t == 0 and half == 0:
                s_f1e.wait(eng, b)
            for m in range(4 * half, 4 * half + 4):
                last = eng.matmul(ps[:, 6 + t // 2, (t % 2) * H:(t % 2) * H + H], hT[:, m, t * P:(t + 1) * P],
                                  ff2T[:, m, :], start=m == 0, stop=m == FM - 1)
            if t % 2 and half:
                s_f2.inc(last)
        elif who == "dve" and t % 2 and half:
            i = t // 2
            s_f2.wait(eng, b, i + 1)
            s_r2.wait(eng, b)
            v = r2[:, 2 * i:2 * i + 2, :]
            s_r3.inc(eng.tensor_tensor(v, ps[:, 6 + i, :].rearrange("p (t h) -> p t h", t=2), v, ALU.add))
            s_r3.wait(eng, b, i + 1)
            last_stats["ln4"] = row_stats(eng, "ln4", r2, i)

    def ln4(who, eng, b):
        normalise(who, eng, b, "ln4", r2, x4, lambda e: (s_xstore.wait(e, b - 1), s_T["ln4"].wait(e, b - 1)))

    def ln4_T(who, eng, b):
        def free(e):
            s_r3.wait(e, b)
        transposes(who, eng, b, "ln4", x4, x4T, (6, 7), None, None, "dve", free)

    def affinity(who, eng, b, chain):
        if who == "pe":
            s_Te["ln4"].wait(eng, b)
            s_Td["ln4"].wait(eng, b)
            for t in range(NT):
                for kd in range(KD):
                    last = eng.matmul(ps[:, 6, t * NE:(t + 1) * NE], x4T[:, kd, t * P:(t + 1) * P], centT[:, kd, :],
                                      start=kd == 0, stop=kd == KD - 1)
            s_af.inc(last)
        elif who == "dve":
            s_af.wait(eng, b)
            s_rk.wait(eng, b - 1)
            d8 = g["desc8"].rearrange("p (t e) -> p t e", t=NT)
            s_afe.inc(eng.tensor_copy(aff[:, :, :], ps[:, 6, 0:NT * NE].rearrange("p (t e) -> p t e", t=NT)))
            s_afe.wait(eng, b)
            chain.link(eng.tensor_reduce(x4[:, :, H], aff[:, :, :], AX.X, ALU.max))
            chain.link(eng.tensor_tensor(ohf[:, :, :], aff[:, :, :],
                                         x4[:, :, H].unsqueeze(2).broadcast_to([P, NT, NE]), ALU.is_equal))
            chain.link(eng.tensor_tensor(ohf[:, :, :], ohf[:, :, :], d8, ALU.mult))
            chain.link(eng.tensor_reduce(amax2[:, :], ohf[:, :, :], AX.X, ALU.max))
            chain.link(eng.tensor_copy(cum[:, 0, :], cum[:, NT, :]))
            s_oh.inc(eng.tensor_tensor(oh[:, :, :], ohf[:, :, :],
                                       amax2[:, :].unsqueeze(2).broadcast_to([P, NT, NE]), ALU.is_equal))
            s_oh.wait(eng, b)
            for t in range(NT):
                chain.link(eng.tensor_tensor(cum[:, t + 1, :], cum[:, t, :], oh[:, t, :], ALU.add))
        elif who == "sp":
            s_oh.wait(eng, b)
            s_xstore.inc(eng.dma_start(xs_dram[bass.ds(b * S, S), :].rearrange("(t p) c -> p t c", p=P), x4[:, :, :]))

    def rank(who, eng, b, chain):
        if who == "pe":
            eng.wait_ge(sem_cf, b * PER_FFN + PER_FFN)
            eng.matmul(ps[:, 1, 0:NT * NE], triu_b[:, :], oh[:, :, :].rearrange("p t e -> p (t e)"),
                       start=True, stop=False)
            s_rk.inc(eng.matmul(ps[:, 1, 0:NT * NE], ones_b[:, :], cum[:, 0:NT, :].rearrange("p t e -> p (t e)"),
                                start=False, stop=True))
        elif who == "dve":
            s_rk.wait(eng, b)
            s_pos.wait(eng, b - 1)
            eb = g["ebase"].rearrange("p (t e) -> p t e", t=NT)
            chain.link(eng.tensor_tensor(posf[:, :, :], ps[:, 1, 0:NT * NE].rearrange("p (t e) -> p t e", t=NT), eb,
                                         ALU.add))
            chain.link(eng.tensor_tensor(posf[:, :, :], posf[:, :, :], oh[:, :, :], ALU.mult))
            chain.link(eng.tensor_reduce(pos1[:, :], posf[:, :, :], AX.X, ALU.add))
            for t in range(NT):
                s_scat[t].wait(eng, b - 1)
            eng.tensor_copy(posi[:, :], pos1[:, :])
            eng.tensor_copy(toki[:, :], tokf[:, :])
            s_pos.inc(eng.tensor_scalar(tokf[:, :], tokf[:, :], float(S), None, ALU.add))

    def scatter_ids(who, eng, b):
        if who == "pool":
            for t in range(NT):
                s_scat[t].wait(eng, b - 1)
            s_pos.wait(eng, b)
            eng.tensor_tensor(spare[:, 3:4], spare[:, 2:3], spare[:, 2:3], ALU.add)
            for t in range(NT):
                s_scat[t].inc(eng.indirect_dma_start(
                    out=table, out_offset=bass.IndirectOffsetOnAxis(ap=posi[:, t:t + 1], axis=0),
                    in_=toki[:, t:t + 1], in_offset=None))

    def keep_warm(who, eng):
        if who == "pe":
            eng.matmul(ps[:, 6, 0:WARM_N], ident, causal[:, 0:WARM_N], start=True, stop=True)

    def iteration(who, eng, i, main, ffn, rk, chains, next_x):
        cm, cf, cr = chains.get("m"), chains.get("f"), chains.get("r")
        f = i - 1
        if who == "dve":
            cm.begin(i)
            cf.begin(f)
            cr.begin(i - 2)
        act_only, others = ("act", None) if who == "act" else (None, who)
        dve_only, not_dve = ("dve", None) if who == "dve" else (None, who)
        units = []
        if ffn:
            units = [lambda m=m: ffn1(who, eng, f, m) for m in range(FM)]
            units += [lambda t=t, h=h: ffn2(who, eng, f, t, h) for t in range(NT) for h in range(2)]
        else:
            units = [lambda: keep_warm(who, eng)] * WARM

        def fill(count):
            for unit in units[:count]:
                unit()
            del units[:count]

        if main:
            if next_x:
                load_x(who, eng, i + 1)
            load_w1(who, eng, i)
            pre2(who, eng, i)
            queries_keys(who, eng, i)
        if rk:
            rank(who, eng, i - 2, cr)
            scatter_ids(who, eng, i - 2)
        if ffn:
            ln3_T(who, eng, f)
        if main:
            values(who, eng, i)
            fill(2)
            for n in range(STEPS + 1):
                inside = n % NT == 0 and n < STEPS
                if n < STEPS:
                    scores(who, eng, i, n, (lambda: fill(1)) if inside and who == "pe" else None)
                if inside and who != "pe":
                    fill(1)
                if n:
                    weigh(who, eng, i, n - 1)
                if n and n % 4 == 0:
                    group_out(act_only, eng, i, n // 4 - 1, cm)
                if n % 4 == 1 and n > 1 and n < STEPS:
                    group_out(others, eng, i, n // 4 - 1, cm)
                if n == 8 and next_x:
                    ln1(who, eng, i + 1, cm)
                    pre_a(who, eng, i + 1)
                if n == 0 or not inside:
                    fill(1)
                if ffn and n == LAST_FILL:
                    assert not units
                    statistics(who, eng, f, "ln4", last_stats.get("ln4"), cf)
            if ffn:
                ln4(who, eng, f)
            if next_x:
                ln1_T(who, eng, i + 1)
            if ffn:
                ln4_T(who, eng, f)
            group_out(others, eng, i, NG - 1, cm)
            if next_x:
                last = sf(who, eng, i + 1, cm)
            ctx_T(who, eng, i, ffn, next_x)
            if ffn:
                affinity(not_dve, eng, f, cf)
            proj_o(who, eng, i, (0, 1, 2))
            if next_x:
                ln2(who, eng, i + 1, last, cm)
                ln2_T(who, eng, i + 1)
            proj_o(who, eng, i, (3,))
            last = add_o(who, eng, i, cm)
            ln3(who, eng, i, last, cm, lambda: ffn and affinity(dve_only, eng, f, cf))
            residual2(who, eng, i)
            if next_x:
                pre_b(who, eng, i + 1)
        else:
            fill(len(units))
            statistics(who, eng, f, "ln4", last_stats.get("ln4"), cf)
            ln4(who, eng, f)
            ln4_T(who, eng, f)
            affinity(who, eng, f, cf)
            if who == "dve":
                cr.end()
                cr.begin(f)
            rank(who, eng, f, cr)
            scatter_ids(who, eng, f)
        if who == "dve":
            if main:
                if not next_x:
                    cm.k += 2
                cm.end()
            if ffn:
                cf.end()
            if rk:
                cr.end()

    def first_constants(who, eng):
        if who in ("dve", "pool"):
            s_load.wait(eng, 0)
        if who == "dve":
            s_fill.wait(eng, 0)
            eng.tensor_copy(triu_b[:, :], tri_u)
            s_pos.inc(eng.tensor_copy(tokf[:, :], g["tok0"]))
            s_const.inc(eng.tensor_tensor(bkm[:, :], col[:, C_ME:C_ME + 2], col[:, C_BK:C_BK + 1].broadcast_to([P, 2]),
                                          ALU.mult))
            s_const.inc(eng.tensor_tensor(sfT[:, :, :], sfT[:, :, :], sfM[:, :, :], ALU.mult))
            s_const.inc(eng.tensor_copy(ohf[:, :, :], g["desc8"].rearrange("p (t e) -> p t e", t=NT)))
            s_const.wait(eng, 0)

    def run(who, eng):
        chains = {}
        if who == "dve":
            chains = {"m": Chain(eng, sem_cm, PER_MAIN), "f": Chain(eng, sem_cf, PER_FFN),
                      "r": Chain(eng, sem_cr, PER_RANK)}
            chains["m"].begin(0)
        cm = chains.get("m")
        ln1(who, eng, 0, cm, lambda: first_constants(who, eng))
        pre_a(who, eng, 0)
        pre_b(who, eng, 0)
        ln1_T(who, eng, 0)
        last = sf(who, eng, 0, cm)
        ln2(who, eng, 0, last, cm)
        ln2_T(who, eng, 0)
        if who == "dve":
            cm.ahead = cm.k
        iteration(who, eng, 0, True, False, False, chains, True)
        if who == "pe":
            s_load_f.wait(eng, 0)
        iteration(who, eng, 1, True, True, False, chains, True)
        with eng.Fori(2, NB - 1) as i:
            iteration(who, eng, i, True, True, True, chains, True)
        iteration(who, eng, NB - 1, True, True, True, chains, False)
        if who == "sp":
            load_w2(eng)
        iteration(who, eng, NB, False, True, True, chains, False)

    def load_w2(eng):
        s_wo.wait(eng, NB - 1)
        s_num.wait(eng, NB - 1)
        s_x2.wait(eng, NB - 1)
        s_r2.wait(eng, NB - 1)
        for e in range(NE):
            g["s_w2"].inc(eng.dma_start(g["arena"][:, e * FM * H:(e + 1) * FM * H], g["w2"][e * P:(e + 1) * P, :]))

    with nc.Block() as block:
        @block.sync
        def _(eng):
            load_x("sp", eng, 0)
            for sig, d, src in ((s_load, con[:, :], g["consts"]), (s_load, col[:, :], g["cols"]),
                                (s_load, sfT[:, :, :], g["sfw"]), (s_load, sfM[:, :, :], g["sfm"]),
                                (s_load, rowb[:, :, :], g["rows"]),
                                (s_load_a, wqT[:, :, :], g["wq"]), (s_load_a, wkT[:, :, :], g["wk"]),
                                (s_load_a, wvT[:, :, :], g["wv"]), (s_load_a, woT[:, :, :], g["wo"]),
                                (s_load_f, ff1T[:, :, :], g["ff1"]), (s_load_f, ff2T[:, :, :], g["ff2"]),
                                (s_load_f, centT[:, :, :], g["cent"]), (s_load_f, slc[:, :], g["slotc"])):
                sig.inc(eng.dma_start(d, src))
            s_fill.wait(eng, 0, 2)
            s_pad.inc(eng.dma_start(xs_dram[N_TOK:N_TOK + P, :], zrow[:, :]))
            run("sp", eng)
            s_xstore.wait(eng, NB - 1)
            s_pad.wait(eng, 0)

        @block.gpsimd
        def _(eng):
            eng.memset(spare[:, 2:4], 0.0)
            s_fill.inc(eng.memset(padid[:, :], N_TOK))
            s_fill.inc(eng.memset(zrow[:, :], 0.0))
            eng.memset(nhalf[:, :], -0.5)
            eng.memset(eps4[:, :], EPS)
            eng.memset(x4[:, :, H:XW], 0.0)
            eng.memset(ones_b[:, :], 1.0)
            eng.memset(vA[:, :, :, D + 1:32], 0.0)
            eng.memset(vA[:, :, :, D:D + 1], 1.0)
            s_fill.inc(eng.memset(cum[:, NT, :], 0.0))
            s_fill.wait(eng, 0)
            w = (NE + 1) * N_TOK // P // NT
            for t in range(NT):
                s_scat[t].inc(eng.dma_start(table.rearrange("(p c) o -> p (c o)", p=P)[:, t * w:(t + 1) * w],
                                            padid[:, t * w:(t + 1) * w]))
            run("pool", eng)
            for t in range(NT):
                s_scat[t].wait(eng, NB - 1)

        @block.scalar
        def _(eng):
            s_fill.wait(eng, 0)
            eng.activation(spare[:, 3:4], spare[:, 2:3], ACT.Identity)
            s_load.wait(eng, 0)
            run("act", eng)

        @block.tensor
        def _(eng):
            s_load.wait(eng, 0)
            s_const.wait(eng, 0)
            s_fill.wait(eng, 0)
            run("pe", eng)
            s_cnt.inc(eng.matmul(ps[0:1, 0, 0:NE], ones_b[:, 0:1], cum[:, NT, :], start=True, stop=True))

        @block.vector
        def _(eng):
            eng.memset(spare[:, 0:2], 0.0)
            run("dve", eng)

            s_load_f.wait(eng, 0)
            s_cnt.wait(eng, 0)
            ch = Chain(eng, sem_ct, 0)
            ch.begin(0)
            o = 0
            k128 = slc[:, o:o + NE * 32].rearrange("p (e k) -> p e k", e=NE)
            o += NE * 32
            le = slc[:, o:o + NE * NE].rearrange("p (e f) -> p e f", e=NE)
            o += NE * NE
            jj = slc[:, o:o + N_SLOT * NE].rearrange("p (j e) -> p j e", e=NE)
            o += N_SLOT * NE
            j1 = slc[:, o:o + N_SLOT]
            ch.link(eng.tensor_copy(cnt[:, :], ps[0:1, 0, 0:NE]))
            t8 = tmp[:, 0:NE * 32].rearrange("p (e k) -> p e k", e=NE)
            ch.link(eng.tensor_tensor(t8, cnt[:, :].unsqueeze(2).broadcast_to([1, NE, 32]), k128, ALU.is_gt))
            ch.link(eng.tensor_reduce(til[:, :], t8, AX.X, ALU.add))
            t8 = tmp[:, 0:NE * NE].rearrange("p (e f) -> p e f", e=NE)
            ch.link(eng.tensor_tensor(t8, til[:, :].unsqueeze(1).broadcast_to([1, NE, NE]), le, ALU.mult))
            ch.link(eng.tensor_reduce(end[:, :], t8, AX.X, ALU.add))
            ind = tmp[:, 0:N_SLOT * NE].rearrange("p (j e) -> p j e", e=NE)
            eb = end[:, :].unsqueeze(1).broadcast_to([1, N_SLOT, NE])
            tabf = g["tabf"]
            ch.link(eng.tensor_tensor(ind, eb, jj, ALU.is_le))
            ch.link(eng.tensor_reduce(tabf[:, 0, :], ind, AX.X, ALU.add))
            ch.link(eng.tensor_tensor(ind, ind, eb, ALU.mult))
            ch.link(eng.tensor_reduce(tabf[:, 1, :], ind, AX.X, ALU.max))
            ch.link(eng.tensor_tensor(tabf[:, 1, :], j1, tabf[:, 1, :], ALU.subtract))
            ch.link(eng.tensor_scalar(tabf[:, 1, :], tabf[:, 1, :], float(P), None, ALU.mult))
            ch.link(eng.scalar_tensor_tensor(out=tabf[:, 1, :], in0=tabf[:, 0, :], scalar=float(N_TOK),
                                             in1=tabf[:, 1, :], op0=ALU.mult, op1=ALU.add))
            ch.link(eng.tensor_scalar(tabf[:, 1, :], tabf[:, 1, :], float(NE * N_TOK), None, ALU.min))
            ch.link(eng.tensor_scalar(tabf[:, 2, :], tabf[:, 0, :], float(NE - 1), float(P), ALU.min, ALU.mult))
            ch.link(eng.tensor_scalar(tabf[:, 0, :], tabf[:, 0, :], float(NE - 1), float(KD * FF), ALU.min, ALU.mult))
            g["s_tab"].inc(eng.tensor_copy(g["tab"][:, :], tabf[:, :, :].rearrange("p a j -> p (a j)")))
            g["s_tab"].wait(eng, 0)


def phase_2(nc, stack, signal, sb_, ps, g):
    def sb(name, shape, dt=F32):
        return sb_(name, shape, dt, stack)

    ident, nhalf, tab, w1_sb = g["ident"], g["nhalf"], g["tab"], g["w1_sb"]
    xs_dram, table, epack, out = g["xs_dram"], g["table"], g["epack"], g["out"]
    spare, eps4 = g["spare"], g["eps4"]
    w2_sb = g["arena"]
    R = range(UN)
    ids = [sb(f"ids{u}", [P, 1], I32) for u in R]
    zero = sb("zero", [P, 1], I32)
    carry = sb("carry", [P, UN])
    ids2 = [sb(f"ids2{u}", [P, 1], I32) for u in R]
    ep = [sb(f"ep{u}", [P, EW]) for u in R]
    xg = [sb(f"xg{u}", [P, XW]) for u in R]
    xx = [sb(f"xx{u}", [P, H]) for u in R]
    ex = [sb(f"ex{u}", [P, 1]) for u in R]
    al = [sb(f"al{u}", [P, 1]) for u in R]
    xh = [sb(f"exh{u}", [P, H]) for u in R]
    xT = [sb(f"exT{u}", [P, KD, P]) for u in R]
    hs = [sb(f"hs{u}", [P, FF]) for u in R]
    hT = [sb(f"ehT{u}", [P, FM, P]) for u in R]
    rr = [sb(f"rr{u}", [P, H]) for u in R]
    oo = [sb(f"oo{u}", [P, H]) for u in R]
    st = [[sb(f"est{k}{u}", [P, 6]) for u in R] for k in range(2)]
    mv = [[sb(f"emv{k}{u}", [P, 2]) for u in R] for k in range(2)]
    rs = [[sb(f"ers{k}{u}", [P, 1]) for u in R] for k in range(2)]

    s_zero = signal("s_zero", 1)
    d_ids = [signal(f"d_ids{u}", 1, 16) for u in R]
    d_ep = [signal(f"d_ep{u}", 1, 16) for u in R]
    d_xg = [signal(f"d_xg{u}", 1, 16) for u in R]
    d_out = [signal(f"d_out{u}", 1, 16) for u in R]
    names = ("ids2", "ex", "xx", "e1", "al", "var0", "eps0", "rs0", "xh", "xT", "xTe", "l1", "l1a", "l1d", "hT",
             "hTa", "hTd", "l2", "y", "r", "var1", "eps1", "rs1", "o", "st0", "st1")
    sg = {n: signal(f"p_{n}", UN) for n in names}

    def wait(eng, n, m, u, ago=0):
        sg[n].wait(eng, m, u + 1 - ago)

    def wait_d(eng, d, m, u, ago=0):
        k = u - ago
        d[k % UN].wait(eng, m + k // UN)

    def at(m, u, ahead):
        k = u + ahead
        return m + k // UN, k % UN

    def fetch_ids(who, eng, m, u):
        if who == "sp":
            j = m * UN + u
            wait(eng, "ids2", m, u, UN)
            wait_d(eng, d_xg, m, u, UN)
            row = eng.value_load(tab[0:1, bass.ds(j + N_SLOT, 1)], min_val=0, max_val=NE * N_TOK)
            d_ids[u].inc(eng.dma_start(ids[u][:, :], table[bass.ds(row, P), :]))

    def fetch_ep(who, eng, m, u):
        if who == "sp":
            j = m * UN + u
            wait(eng, "y", m, u, UN)
            wait(eng, "hTa", m, u, UN)
            row = eng.value_load(tab[0:1, bass.ds(j + 2 * N_SLOT, 1)], min_val=0, max_val=(NE - 1) * P)
            d_ep[u].inc(eng.dma_start(ep[u][:, :], epack[bass.ds(row, P), :]))

    def gather(who, eng, m, u):
        if who == "pool":
            wait_d(eng, d_ids, m, u)
            wait(eng, "xh", m, u, UN)
            wait(eng, "xx", m, u, UN)
            eng.tensor_tensor(carry[:, u:u + 1], spare[:, 2:3], spare[:, 2:3], ALU.add)
            d_xg[u].inc(eng.indirect_dma_start(out=xg[u][:, :], out_offset=None, in_=xs_dram,
                                               in_offset=bass.IndirectOffsetOnAxis(ap=ids[u][:, :], axis=0)))

    def stats(who, eng, m, u, k, src, dst, done, ready):
        if who == "dve":
            sg[f"st{k}"].inc(eng.bn_stats(st[k][u][:, :], src))
            wait(eng, f"st{k}", m, u)
            eng.tensor_copy(spare[:, 1:2], spare[:, 0:1])
            sg[f"var{k}"].inc(eng.bn_aggr(mv[k][u][:, :], st[k][u][:, :]))
            wait(eng, f"rs{k}", m, u)
            ready(eng)
            sg[done].inc(eng.tensor_scalar(dst, src, mv[k][u][:, 0:1], rs[k][u][:, :], ALU.subtract, ALU.mult))
        elif who == "pool":
            wait(eng, f"var{k}", m, u)
            sg[f"eps{k}"].inc(eng.tensor_tensor(rs[k][u][:, :], mv[k][u][:, 1:2], eps4[:, 0:1], ALU.add))
            wait(eng, f"eps{k}", m, u)
            sg[f"rs{k}"].inc(eng.tensor_tensor(rs[k][u][:, :], rs[k][u][:, :], nhalf[:, 0:1], ALU.pow))

    def norm(who, eng, m, u):
        if who in ("dve", "act"):
            wait_d(eng, d_xg, m, u)
        stats(who, eng, m, u, 0, xg[u][:, 0:H], xh[u][:, :], "xh", lambda e: wait(e, "xT", m, u, UN))
        if who == "act":
            wait(eng, "al", m, u, UN)
            sg["ex"].inc(eng.activation(ex[u][:, :], xg[u][:, H:H + 1], ACT.Exp, scale=-1.0))
            wait(eng, "r", m, u, UN)
            sg["xx"].inc(eng.activation(xx[u][:, :], xg[u][:, 0:H], ACT.Copy, scale=2.0))
        elif who == "dve":
            wait(eng, "ex", m, u)
            sg["e1"].inc(eng.tensor_scalar(al[u][:, :], ex[u][:, :], 1.0, None, ALU.add))
            wait(eng, "e1", m, u)
            sg["al"].inc(eng.reciprocal(al[u][:, :], al[u][:, :]))

    def keep_ids(who, eng, m, u):
        if who == "pool":
            wait_d(eng, d_out, m, u, UN)
            sg["ids2"].inc(eng.tensor_tensor(ids2[u][:, :], ids[u][:, :], zero[:, :], ALU.add))

    def x_T(who, eng, m, u):
        if who == "pe":
            wait(eng, "xh", m, u)
            wait(eng, "xTe", m, u, 1)
            for kd in range(KD):
                last = eng.transpose(ps[:, 6, kd * P:(kd + 1) * P], xh[u][:, kd * P:(kd + 1) * P], ident)
            sg["xT"].inc(last)
        elif who == "act":
            wait(eng, "xT", m, u)
            wait_d(eng, d_ep, m, u)
            wait(eng, "l1", m, u, UN)
            for kd in range(KD):
                last = eng.activation(xT[u][:, kd, :], ps[:, 6, kd * P:(kd + 1) * P], ACT.Identity,
                                      bias=ep[u][:, E_B + kd:E_B + kd + 1], scale=ep[u][:, E_G + kd:E_G + kd + 1])
            sg["xTe"].inc(last)

    def layer1(who, eng, m, u):
        if who == "pe":
            col = eng.value_load(tab[0:1, bass.ds(m * UN + u, 1)], min_val=0, max_val=(NE - 1) * KD * FF)
            wait(eng, "xTe", m, u)
            wait(eng, "l1a", m, u, 1)
            wait(eng, "l1d", m, u, 1)
            for half in range(2):
                for kd in range(KD):
                    last = eng.matmul(ps[:, half, :], xT[u][:, kd, :],
                                      w1_sb[:, bass.ds(col + (kd * FF + half * 512), 512)],
                                      start=kd == 0, stop=kd == KD - 1)
            sg["l1"].inc(last)
        elif who == "act":
            wait(eng, "l1", m, u)
            wait(eng, "hT", m, u, UN)
            sg["l1a"].inc(eng.activation(hs[u][:, 0:512], ps[:, 0, :], ACT.Copy))
        elif who == "dve":
            wait(eng, "l1", m, u)
            wait(eng, "hT", m, u, UN)
            sg["l1d"].inc(eng.tensor_copy(hs[u][:, 512:1024], ps[:, 1, :]))

    def hidden_T(who, eng, m, u):
        if who == "pe":
            wait(eng, "l1a", m, u)
            wait(eng, "l1d", m, u)
            wait(eng, "hTa", m, u, 1)
            wait(eng, "hTd", m, u, 1)
            for f in range(FM):
                last = eng.transpose(ps[:, 2 + f // 4, (f % 4) * P:(f % 4 + 1) * P], hs[u][:, f * P:(f + 1) * P], ident)
            sg["hT"].inc(last)
        elif who in ("act", "dve"):
            wait(eng, "hT", m, u)
            wait(eng, "l2", m, u, UN)
            f0 = 0 if who == "act" else 4
            for f in range(f0, f0 + 4):
                o, i = hT[u][:, f, :], ps[:, 2 + f // 4, (f % 4) * P:(f % 4 + 1) * P]
                bias = ep[u][:, E_B1 + f:E_B1 + f + 1]
                if who == "act":
                    last = eng.activation(o, i, ACT.Relu, bias=bias)
                else:
                    last = eng.tensor_scalar(o, i, bias, 0.0, ALU.add, ALU.max)
            sg["hTa" if who == "act" else "hTd"].inc(last)

    def layer2(who, eng, m, u, between=None):
        if who == "pe":
            col = eng.value_load(tab[0:1, bass.ds(m * UN + u, 1)], min_val=0, max_val=(NE - 1) * FM * H)
            wait(eng, "hTa", m, u)
            wait(eng, "hTd", m, u)
            wait(eng, "y", m, u, 1)
            for f in range(FM):
                if f == FM - 1 and between:
                    between()
                last = eng.matmul(ps[:, 4, 0:H], hT[u][:, f, :], w2_sb[:, bass.ds(col + f * H, H)],
                                  start=f == 0, stop=f == FM - 1)
            sg["l2"].inc(last)
        elif who == "dve":
            wait(eng, "l2", m, u)
            sg["y"].inc(eng.tensor_tensor(rr[u][:, :], ps[:, 4, 0:H], ep[u][:, E_B2:E_B2 + H], ALU.add))

    def finish(who, eng, m, u):
        if who == "dve":
            wait(eng, "xx", m, u)
            wait(eng, "al", m, u)
            wait(eng, "y", m, u)
            sg["r"].inc(eng.scalar_tensor_tensor(out=rr[u][:, :], in0=rr[u][:, :], scalar=al[u][:, :], in1=xx[u][:, :],
                                                 op0=ALU.mult, op1=ALU.add))
            wait(eng, "r", m, u)
        stats(who, eng, m, u, 1, rr[u][:, :], oo[u][:, :], "o", lambda e: wait_d(e, d_out, m, u, UN))

    def scatter(who, eng, m, u):
        if who == "pool":
            wait(eng, "o", m, u)
            eng.tensor_tensor(spare[:, 3:4], spare[:, 2:3], spare[:, 2:3], ALU.add)
            d_out[u].inc(eng.indirect_dma_start(out=out, out_offset=bass.IndirectOffsetOnAxis(ap=ids2[u][:, :], axis=0),
                                                in_=oo[u][:, :], in_offset=None, bounds_check=N_TOK - 1,
                                                oob_is_err=False))

    def slot(who, eng, m, u, first=False, last=False):
        left = UN - 1 - u if last else UN * N_SLOT
        if left >= 3:
            fetch_ids(who, eng, *at(m, u, 3))
        layer1(who, eng, m, u)
        if left >= 1:
            norm(who, eng, *at(m, u, 1))
        if not first or u > 1:
            scatter(who, eng, *at(m, u, -2))
        if left >= 3:
            gather(who, eng, *at(m, u, 3))
        if who == "pe" and (not first or u):
            layer2(who, eng, *at(m, u, -1), (lambda: x_T(who, eng, *at(m, u, 1))) if left >= 1 else None)
        elif left >= 1:
            x_T(who, eng, *at(m, u, 1))
        if who != "pe" and (not first or u):
            layer2(who, eng, *at(m, u, -1))
        hidden_T(who, eng, m, u)
        if not first or u:
            finish(who, eng, *at(m, u, -1))
        if left >= 2:
            fetch_ep(who, eng, *at(m, u, 2))
        if left >= 1:
            keep_ids(who, eng, *at(m, u, 1))

    def run(who, eng):
        M = N_SLOT // UN
        for u in range(3):
            fetch_ids(who, eng, 0, u)
        for u in range(2):
            fetch_ep(who, eng, 0, u)
        for u in range(3):
            gather(who, eng, 0, u)
        norm(who, eng, 0, 0)
        keep_ids(who, eng, 0, 0)
        x_T(who, eng, 0, 0)
        for u in R:
            slot(who, eng, 0, u, first=True)
        with eng.Fori(1, M - 1) as m:
            for u in R:
                slot(who, eng, m, u)
        for u in R:
            slot(who, eng, M - 1, u, last=True)
        layer2(who, eng, M - 1, UN - 1)
        scatter(who, eng, M - 1, UN - 2)
        finish(who, eng, M - 1, UN - 1)
        scatter(who, eng, M - 1, UN - 1)
        if who == "pool":
            for u in R:
                d_out[u].wait(eng, M - 1)

    with nc.Block() as block:
        @block.sync
        def _(eng):
            run("sp", eng)

        @block.gpsimd
        def _(eng):
            s_zero.inc(eng.memset(zero[:, :], 0))
            s_zero.wait(eng, 0)
            run("pool", eng)

        @block.scalar
        def _(eng):
            run("act", eng)

        @block.tensor
        def _(eng):
            g["s_w1"].wait(eng, 0)
            g["s_w2"].wait(eng, 0)
            run("pe", eng)

        @block.vector
        def _(eng):
            run("dve", eng)


def kernel(**inputs):
    import numpy as np
    import concourse.bacc as bacc
    from concourse.bass_utils import run_bass_kernel_spmd

    a = {k: np.asarray(v) for k, v in inputs.items()}

    def by_rows(w):
        return np.ascontiguousarray(w.T.reshape(-1, P, w.shape[0]).transpose(1, 0, 2))

    def column(v):
        return v.reshape(-1, P).T

    f32 = np.float32
    c = "L0_attn_"
    half = (np.arange(P) // D % 2)[:, None]
    scale = f32(D ** -0.5)
    cols = np.concatenate([column(a[c + n]) for n in ("g1", "b1", "g2", "b2", "g3", "b3", "bq", "bk", "ff1_b")]
                          + [(half == 0) * scale, (half == 1) * scale], axis=1).astype(f32)
    rows = np.stack([np.broadcast_to(a[c + n], (P, H)) for n in ("sf_b", "bo", "ff2_b", "bv")], axis=1)
    i = np.arange(P)
    e = np.arange(NE)
    consts = np.concatenate([
        np.eye(P), i[:, None] < i[None, :], i[:, None] <= np.arange(S)[None, :],
        np.broadcast_to(np.tile(NE - e, NT), (P, NT * NE)), np.broadcast_to(np.tile(e * N_TOK, NT), (P, NT * NE)),
        i[:, None] + P * np.arange(NT)[None, :]], axis=1).astype(f32)
    slotc = np.concatenate([np.tile(P * np.arange(32), NE), np.tril(np.ones((NE, NE))).ravel(),
                            np.repeat(np.arange(N_SLOT), NE), np.arange(N_SLOT)])[None, :].astype(f32)
    f = "L0_ffn_"
    w1 = np.concatenate([by_rows(w).reshape(P, -1) for w in a[f + "w1"]], axis=0)
    w2 = np.concatenate([by_rows(w).reshape(P, -1) for w in a[f + "w2"]], axis=0)
    epack = np.concatenate([np.concatenate([column(a[f + "ln_g"][k]), column(a[f + "ln_b"][k]),
                                            column(a[f + "b1"][k]), np.broadcast_to(a[f + "b2"][k], (P, H))], axis=1)
                            for k in range(NE)], axis=0)
    arrays = dict(x=a[c + "x"].reshape(N_TOK, H), sfw=by_rows(a[c + "sf_w"]), sfm=by_rows(a[c + "mask"]),
                  wq=by_rows(a[c + "wq"]), wk=by_rows(a[c + "wk"]), wv=by_rows(a[c + "wv"]), wo=by_rows(a[c + "wo"]),
                  ff1=by_rows(a[c + "ff1_w"]), ff2=by_rows(a[c + "ff2_w"]), cent=by_rows(a[f + "centroids"]),
                  rows=rows, cols=cols, consts=consts, slotc=slotc, w1=w1, w2=w2, epack=epack)
    nc = bacc.Bacc("TRN2", target_bir_lowering=False, num_devices=1)
    args, feed = [], {}
    for name, v in arrays.items():
        v = np.ascontiguousarray(v)
        feed[f"in_{name}"] = v
        args.append(nc.dram_tensor(f"in_{name}", v.shape, mybir.dt.from_np(v.dtype), kind="ExternalInput").ap())
    out = nc.dram_tensor("out_y", (N_TOK, H), F32, kind="ExternalOutput").ap()
    build(nc, *args, out)
    r = run_bass_kernel_spmd(nc, [feed], core_ids=[0])
    return r.results[0]["out_y"].reshape(NB, S, H)
```
